# Optimizing a Trainium2 kernel written in Bass

```python
import numpy as np
import jax
import jax.numpy as jnp

def _softmax(x, axis=-1):
    return jax.nn.softmax(x, axis=axis)

def _gelu(x):
    return jax.nn.gelu(x, approximate=True)

def _silu(x):
    return jax.nn.silu(x)

def _sigmoid(x):
    return jax.nn.sigmoid(x)

def _layernorm(x, axis=-1, eps=1e-05):
    m = jnp.mean(x, axis=axis, keepdims=True)
    v = jnp.var(x, axis=axis, keepdims=True)
    return (x - m) / jnp.sqrt(v + eps)

def _scatter_add(tgt, idx, src, axis=0):
    return tgt.at[idx].add(src)

def _segment_sum(src, seg, n):
    return jax.ops.segment_sum(src, seg, n)
kernel_name = 'mk_xattn_ffn_d1_seqx_r4_2c03c5'

def setup_inputs(seed: int=0):
    np.random.seed(seed)
    _w = jnp.asarray

    def _rec_inputs():
        import jax
        import jax.numpy as jnp
        _rk = jax.random.key(seed)
        x = -0.0003929 + 0.9999 * jax.random.normal(jax.random.fold_in(_rk, 1), (2, 512, 1024), jnp.float32)
        _lenS = 512 - jax.random.randint(jax.random.fold_in(_rk, 7), (2,), 0, max(1, 512 // 4) + 1, jnp.int32)
        _lenS2 = 1024 - jax.random.randint(jax.random.fold_in(_rk, 8), (2,), 0, max(1, 1024 // 4) + 1, jnp.int32)
        pos_BxS = jnp.broadcast_to(jnp.arange(512, dtype=jnp.int32), (2, 512))
        _ctx_1024P = jax.random.normal(jax.random.fold_in(_rk, 12), (2, 16, 256), jnp.float32)
        _ctx_1024c = jax.random.dirichlet(jax.random.fold_in(_rk, 512), 0.3 * jnp.ones((16,), jnp.float32), (2, 1024))
        _ctx_1024t = jnp.einsum('bsk,bkd->bsd', _ctx_1024c, _ctx_1024P)
        _ctx_1024t = _ctx_1024t * jax.lax.rsqrt(jnp.mean(jnp.square(_ctx_1024t)) + 1e-12) * 0.953939
        ctx_1024 = 6.77073e-06 + 0.0199965 * (_ctx_1024t + 0.3 * jax.random.normal(jax.random.fold_in(_rk, 612), (2, 1024, 256), jnp.float32))
        return (x, pos_BxS, ctx_1024)
    x, pos_BxS, ctx_1024 = _rec_inputs()

    def _L0_xattn_setup():
        import jax, jax.numpy as jnp
        import numpy as np
        H = 256
        C = 4
        RH = 16
        HS = H // RH
        DR = 8
        M = 1024
        NH = 16
        HD = H // NH
        A_SIZE = (C - 1) * RH
        B_SIZE = C * RH
        EPS = 1e-05
        SSM_EPS = 1e-05

        def rat_read(res, W, gamma, beta, num_outputs):
            b, l, _ = res.shape
            x = res.reshape(b, l, H, C)
            y = jnp.einsum('blhc,hoc->bloh', x, W)
            mu = y.mean(-1, keepdims=True)
            var = y.var(-1, keepdims=True)
            yn = (y - mu) * jax.lax.rsqrt(var + EPS)
            yn = yn * gamma.reshape(num_outputs, H) + beta.reshape(num_outputs, H)
            return yn.reshape(b, l, num_outputs * H)

        def rope(x, pos):
            half = HD // 2
            inv = 1.0 / 10000.0 ** (jnp.arange(half, dtype=jnp.float32) / half)
            ang = pos.astype(jnp.float32)[..., None] * inv
            cos = jnp.cos(ang)[:, :, None, :]
            sin = jnp.sin(ang)[:, :, None, :]
            x1, x2 = (x[..., :half], x[..., half:])
            return jnp.concatenate([x1 * cos - x2 * sin, x2 * cos + x1 * sin], axis=-1)

        def attention(qkv_in, qkv_w, pos):
            b, l, _ = qkv_in.shape
            q, k, v = jnp.split(qkv_in, 3, axis=-1)
            q = jnp.einsum('bli,oi->blo', q, qkv_w[0]).reshape(b, l, NH, HD)
            k = jnp.einsum('bli,oi->blo', k, qkv_w[1]).reshape(b, l, NH, HD)
            v = jnp.einsum('bli,oi->blo', v, qkv_w[2]).reshape(b, l, NH, HD)
            q = rope(q, pos)
            k = rope(k, pos)
            scores = jnp.einsum('bqhd,bkhd->bhqk', q, k) / np.sqrt(HD).astype(np.float32)
            mask = jnp.tril(jnp.ones((l, l), dtype=bool))
            scores = jnp.where(mask, scores, jnp.float32(-1e+30))
            p = jax.nn.softmax(scores, axis=-1)
            o = jnp.einsum('bhqk,bkhd->bqhd', p, v)
            return o.reshape(b, l, H)

        def rat_write(res, y, wod_w, wab_w, wab_b, du_w, du_b):
            b, l, _ = res.shape
            o_d = y @ wod_w.T
            A_B = y @ wab_w.T + wab_b
            out = o_d[..., :H]
            delta_low = o_d[..., H:]
            A_logit = A_B[..., :A_SIZE]
            B_proj = A_B[..., A_SIZE:2 * A_SIZE]
            B_skip = A_B[..., 2 * A_SIZE:]
            delta = jax.nn.softplus(delta_low @ du_w.T + du_b)
            hs = res.reshape(b, l, HS, RH, C)
            out = out.reshape(b, l, HS, RH, 1)
            delta = delta.reshape(b, l, HS, RH, 1)
            A_logit = A_logit.reshape(b, l, 1, RH, C - 1)
            B_proj = B_proj.reshape(b, l, 1, RH, C - 1)
            B_skip = B_skip.reshape(b, l, 1, RH, 1)
            A_neg = -jax.nn.softplus(A_logit)
            A_bar = jnp.exp(delta * A_neg)
            B_bar = (A_bar - 1.0) / (A_neg - SSM_EPS) * B_proj
            B_bar_skip = delta * B_skip
            A_full = jnp.concatenate([A_bar, jnp.ones_like(A_bar[..., :1])], axis=-1)
            B_full = jnp.concatenate([B_bar, B_bar_skip], axis=-1)
            return (hs * A_full + out * B_full).reshape(b, l, H * C)

        def layer_forward(hidden_states, position_ids, attn_read_w, attn_read_g, attn_read_b, qkv_w, attn_wod_w, attn_wab_w, attn_wab_b, attn_du_w, attn_du_b, mlp_read_w, mlp_read_g, mlp_read_b, mlp_in_w, mlp_wod_w, mlp_wab_w, mlp_wab_b, mlp_du_w, mlp_du_b):
            qkv_in = rat_read(hidden_states, attn_read_w, attn_read_g, attn_read_b, 3)
            attn_out = attention(qkv_in, qkv_w, position_ids)
            hidden_states = rat_write(hidden_states, attn_out, attn_wod_w, attn_wab_w, attn_wab_b, attn_du_w, attn_du_b)
            mlp_in = rat_read(hidden_states, mlp_read_w, mlp_read_g, mlp_read_b, 2)
            g_in, u_in = (mlp_in[..., :H], mlp_in[..., H:])
            gate = jnp.einsum('bli,oi->blo', g_in, mlp_in_w[0])
            up = jnp.einsum('bli,oi->blo', u_in, mlp_in_w[1])
            mlp_out = jax.nn.silu(gate) * up
            hidden_states = rat_write(hidden_states, mlp_out, mlp_wod_w, mlp_wab_w, mlp_wab_b, mlp_du_w, mlp_du_b)
            return hidden_states
        key = jax.random.key(seed)
        ks = jax.random.split(key, 20)
        B, L = (2, 512)
        s = 0.02
        return {'hidden_states': jax.random.normal(ks[0], (B, L, H * C), jnp.float32), 'position_ids': jnp.tile(jnp.arange(L, dtype=jnp.int64), (B, 1)), 'attn_read_w': jax.random.normal(ks[1], (H, 3, C), jnp.float32) / np.sqrt(C).astype(np.float32), 'attn_read_g': jnp.ones((3 * H,), jnp.float32), 'attn_read_b': jnp.zeros((3 * H,), jnp.float32), 'qkv_w': jax.random.normal(ks[2], (3, H, H), jnp.float32) * s, 'attn_wod_w': jax.random.normal(ks[3], (H + DR, H), jnp.float32) * s, 'attn_wab_w': jax.random.normal(ks[4], (A_SIZE + B_SIZE, H), jnp.float32) * s, 'attn_wab_b': jax.random.normal(ks[5], (A_SIZE + B_SIZE,), jnp.float32) * s, 'attn_du_w': jax.random.normal(ks[6], (H, DR), jnp.float32) * s, 'attn_du_b': jax.random.normal(ks[7], (H,), jnp.float32) * s, 'mlp_read_w': jax.random.normal(ks[8], (H, 2, C), jnp.float32) / np.sqrt(C).astype(np.float32), 'mlp_read_g': jnp.ones((2 * H,), jnp.float32), 'mlp_read_b': jnp.zeros((2 * H,), jnp.float32), 'mlp_in_w': jax.random.normal(ks[9], (2, M, H), jnp.float32) * s, 'mlp_wod_w': jax.random.normal(ks[10], (H + DR, M), jnp.float32) * s, 'mlp_wab_w': jax.random.normal(ks[11], (A_SIZE + B_SIZE, M), jnp.float32) * s, 'mlp_wab_b': jax.random.normal(ks[12], (A_SIZE + B_SIZE,), jnp.float32) * s, 'mlp_du_w': jax.random.normal(ks[13], (H, DR), jnp.float32) * s, 'mlp_du_b': jax.random.normal(ks[14], (H,), jnp.float32) * s}
    _L0_xattn_all = _L0_xattn_setup()
    _L0_xattn_in = {k: v for k, v in _L0_xattn_all.items() if k in ('attn_read_w', 'attn_read_g', 'attn_read_b', 'qkv_w', 'attn_wod_w', 'attn_wab_w', 'attn_wab_b', 'attn_du_w', 'attn_du_b', 'mlp_read_w', 'mlp_read_g', 'mlp_read_b', 'mlp_wod_w', 'mlp_wab_w', 'mlp_wab_b', 'mlp_du_w', 'mlp_du_b')}
    del _L0_xattn_all

    def _L0_ffn_setup():
        import jax, jax.numpy as jnp
        import numpy as np
        HID, INTER = (1024, 3584)
        B, S = (2, 512)

        def _binary_diff_weight(w, base):
            d = w - base
            coeff = jnp.mean(jnp.abs(d))
            return base + coeff * jnp.sign(d)
        key = jax.random.key(seed)
        ks = jax.random.split(key, 7)
        return {'hidden_states': jax.random.normal(ks[0], (B, S, HID), dtype=jnp.float32), 'w1': jax.random.normal(ks[1], (INTER, HID), dtype=jnp.float32) * 0.02, 'mean_w1': jax.random.normal(ks[2], (INTER, HID), dtype=jnp.float32) * 0.02, 'w2': jax.random.normal(ks[3], (HID, INTER), dtype=jnp.float32) * 0.02, 'mean_w2': jax.random.normal(ks[4], (HID, INTER), dtype=jnp.float32) * 0.02, 'w3': jax.random.normal(ks[5], (INTER, HID), dtype=jnp.float32) * 0.02, 'mean_w3': jax.random.normal(ks[6], (INTER, HID), dtype=jnp.float32) * 0.02}
    _L0_ffn_all = _L0_ffn_setup()
    _L0_ffn_in = {k: v for k, v in _L0_ffn_all.items() if k in ('w1', 'mean_w1', 'w2', 'mean_w2', 'w3', 'mean_w3')}
    del _L0_ffn_all
    return {'x': x, 'pos_BxS': pos_BxS, 'ctx_1024': ctx_1024, 'L0_xattn_attn_read_w': _L0_xattn_in['attn_read_w'], 'L0_xattn_attn_read_g': _L0_xattn_in['attn_read_g'], 'L0_xattn_attn_read_b': _L0_xattn_in['attn_read_b'], 'L0_xattn_qkv_w': _L0_xattn_in['qkv_w'], 'L0_xattn_attn_wod_w': _L0_xattn_in['attn_wod_w'], 'L0_xattn_attn_wab_w': _L0_xattn_in['attn_wab_w'], 'L0_xattn_attn_wab_b': _L0_xattn_in['attn_wab_b'], 'L0_xattn_attn_du_w': _L0_xattn_in['attn_du_w'], 'L0_xattn_attn_du_b': _L0_xattn_in['attn_du_b'], 'L0_xattn_mlp_read_w': _L0_xattn_in['mlp_read_w'], 'L0_xattn_mlp_read_g': _L0_xattn_in['mlp_read_g'], 'L0_xattn_mlp_read_b': _L0_xattn_in['mlp_read_b'], 'L0_xattn_mlp_wod_w': _L0_xattn_in['mlp_wod_w'], 'L0_xattn_mlp_wab_w': _L0_xattn_in['mlp_wab_w'], 'L0_xattn_mlp_wab_b': _L0_xattn_in['mlp_wab_b'], 'L0_xattn_mlp_du_w': _L0_xattn_in['mlp_du_w'], 'L0_xattn_mlp_du_b': _L0_xattn_in['mlp_du_b'], 'L0_ffn_w1': _L0_ffn_in['w1'], 'L0_ffn_mean_w1': _L0_ffn_in['mean_w1'], 'L0_ffn_w2': _L0_ffn_in['w2'], 'L0_ffn_mean_w2': _L0_ffn_in['mean_w2'], 'L0_ffn_w3': _L0_ffn_in['w3'], 'L0_ffn_mean_w3': _L0_ffn_in['mean_w3']}

def reference(x, pos_BxS, ctx_1024, L0_xattn_attn_read_w, L0_xattn_attn_read_g, L0_xattn_attn_read_b, L0_xattn_qkv_w, L0_xattn_attn_wod_w, L0_xattn_attn_wab_w, L0_xattn_attn_wab_b, L0_xattn_attn_du_w, L0_xattn_attn_du_b, L0_xattn_mlp_read_w, L0_xattn_mlp_read_g, L0_xattn_mlp_read_b, L0_xattn_mlp_wod_w, L0_xattn_mlp_wab_w, L0_xattn_mlp_wab_b, L0_xattn_mlp_du_w, L0_xattn_mlp_du_b, L0_ffn_w1, L0_ffn_mean_w1, L0_ffn_w2, L0_ffn_mean_w2, L0_ffn_w3, L0_ffn_mean_w3):
    import jax
    import jax.numpy as jnp

    def _L0_xattn_ref(hidden_states, position_ids, attn_read_w, attn_read_g, attn_read_b, qkv_w, attn_wod_w, attn_wab_w, attn_wab_b, attn_du_w, attn_du_b, mlp_read_w, mlp_read_g, mlp_read_b, mlp_in_w, mlp_wod_w, mlp_wab_w, mlp_wab_b, mlp_du_w, mlp_du_b):
        import jax, jax.numpy as jnp
        import numpy as np
        H = 256
        C = 4
        RH = 16
        HS = H // RH
        DR = 8
        M = 1024
        NH = 16
        HD = H // NH
        A_SIZE = (C - 1) * RH
        B_SIZE = C * RH
        EPS = 1e-05
        SSM_EPS = 1e-05

        def rat_read(res, W, gamma, beta, num_outputs):
            b, l, _ = res.shape
            x = res.reshape(b, l, H, C)
            y = jnp.einsum('blhc,hoc->bloh', x, W)
            mu = y.mean(-1, keepdims=True)
            var = y.var(-1, keepdims=True)
            yn = (y - mu) * jax.lax.rsqrt(var + EPS)
            yn = yn * gamma.reshape(num_outputs, H) + beta.reshape(num_outputs, H)
            return yn.reshape(b, l, num_outputs * H)

        def rope(x, pos):
            half = HD // 2
            inv = 1.0 / 10000.0 ** (jnp.arange(half, dtype=jnp.float32) / half)
            ang = pos.astype(jnp.float32)[..., None] * inv
            cos = jnp.cos(ang)[:, :, None, :]
            sin = jnp.sin(ang)[:, :, None, :]
            x1, x2 = (x[..., :half], x[..., half:])
            return jnp.concatenate([x1 * cos - x2 * sin, x2 * cos + x1 * sin], axis=-1)

        def attention(qkv_in, qkv_w, pos):
            b, l, _ = qkv_in.shape
            q, k, v = jnp.split(qkv_in, 3, axis=-1)
            q = jnp.einsum('bli,oi->blo', q, qkv_w[0]).reshape(b, l, NH, HD)
            k = jnp.einsum('bli,oi->blo', k, qkv_w[1]).reshape(b, l, NH, HD)
            v = jnp.einsum('bli,oi->blo', v, qkv_w[2]).reshape(b, l, NH, HD)
            q = rope(q, pos)
            k = rope(k, pos)
            scores = jnp.einsum('bqhd,bkhd->bhqk', q, k) / np.sqrt(HD).astype(np.float32)
            mask = jnp.tril(jnp.ones((l, l), dtype=bool))
            scores = jnp.where(mask, scores, jnp.float32(-1e+30))
            p = jax.nn.softmax(scores, axis=-1)
            o = jnp.einsum('bhqk,bkhd->bqhd', p, v)
            return o.reshape(b, l, H)

        def rat_write(res, y, wod_w, wab_w, wab_b, du_w, du_b):
            b, l, _ = res.shape
            o_d = y @ wod_w.T
            A_B = y @ wab_w.T + wab_b
            out = o_d[..., :H]
            delta_low = o_d[..., H:]
            A_logit = A_B[..., :A_SIZE]
            B_proj = A_B[..., A_SIZE:2 * A_SIZE]
            B_skip = A_B[..., 2 * A_SIZE:]
            delta = jax.nn.softplus(delta_low @ du_w.T + du_b)
            hs = res.reshape(b, l, HS, RH, C)
            out = out.reshape(b, l, HS, RH, 1)
            delta = delta.reshape(b, l, HS, RH, 1)
            A_logit = A_logit.reshape(b, l, 1, RH, C - 1)
            B_proj = B_proj.reshape(b, l, 1, RH, C - 1)
            B_skip = B_skip.reshape(b, l, 1, RH, 1)
            A_neg = -jax.nn.softplus(A_logit)
            A_bar = jnp.exp(delta * A_neg)
            B_bar = (A_bar - 1.0) / (A_neg - SSM_EPS) * B_proj
            B_bar_skip = delta * B_skip
            A_full = jnp.concatenate([A_bar, jnp.ones_like(A_bar[..., :1])], axis=-1)
            B_full = jnp.concatenate([B_bar, B_bar_skip], axis=-1)
            return (hs * A_full + out * B_full).reshape(b, l, H * C)

        def layer_forward(hidden_states, position_ids, attn_read_w, attn_read_g, attn_read_b, qkv_w, attn_wod_w, attn_wab_w, attn_wab_b, attn_du_w, attn_du_b, mlp_read_w, mlp_read_g, mlp_read_b, mlp_in_w, mlp_wod_w, mlp_wab_w, mlp_wab_b, mlp_du_w, mlp_du_b):
            qkv_in = rat_read(hidden_states, attn_read_w, attn_read_g, attn_read_b, 3)
            attn_out = attention(qkv_in, qkv_w, position_ids)
            hidden_states = rat_write(hidden_states, attn_out, attn_wod_w, attn_wab_w, attn_wab_b, attn_du_w, attn_du_b)
            mlp_in = rat_read(hidden_states, mlp_read_w, mlp_read_g, mlp_read_b, 2)
            g_in, u_in = (mlp_in[..., :H], mlp_in[..., H:])
            gate = jnp.einsum('bli,oi->blo', g_in, mlp_in_w[0])
            up = jnp.einsum('bli,oi->blo', u_in, mlp_in_w[1])
            mlp_out = jax.nn.silu(gate) * up
            hidden_states = rat_write(hidden_states, mlp_out, mlp_wod_w, mlp_wab_w, mlp_wab_b, mlp_du_w, mlp_du_b)
            return hidden_states
        return layer_forward(hidden_states, position_ids, attn_read_w, attn_read_g, attn_read_b, qkv_w, attn_wod_w, attn_wab_w, attn_wab_b, attn_du_w, attn_du_b, mlp_read_w, mlp_read_g, mlp_read_b, mlp_in_w, mlp_wod_w, mlp_wab_w, mlp_wab_b, mlp_du_w, mlp_du_b)

    def _L0_ffn_ref(hidden_states, w1, mean_w1, w2, mean_w2, w3, mean_w3):
        import jax, jax.numpy as jnp
        import numpy as np
        HID, INTER = (1024, 3584)
        B, S = (2, 512)

        def _binary_diff_weight(w, base):
            d = w - base
            coeff = jnp.mean(jnp.abs(d))
            return base + coeff * jnp.sign(d)
        W1 = _binary_diff_weight(w1, mean_w1)
        W2 = _binary_diff_weight(w2, mean_w2)
        W3 = _binary_diff_weight(w3, mean_w3)
        gate = jnp.einsum('bsh,ih->bsi', hidden_states, W1)
        up = jnp.einsum('bsh,ih->bsi', hidden_states, W3)
        h = jax.nn.silu(gate) * up
        return jnp.einsum('bsi,hi->bsh', h, W2)
    x = x + _L0_xattn_ref(_layernorm(x, axis=-1), pos_BxS, L0_xattn_attn_read_w, L0_xattn_attn_read_g, L0_xattn_attn_read_b, L0_xattn_qkv_w, L0_xattn_attn_wod_w, L0_xattn_attn_wab_w, L0_xattn_attn_wab_b, L0_xattn_attn_du_w, L0_xattn_attn_du_b, L0_xattn_mlp_read_w, L0_xattn_mlp_read_g, L0_xattn_mlp_read_b, ctx_1024, L0_xattn_mlp_wod_w, L0_xattn_mlp_wab_w, L0_xattn_mlp_wab_b, L0_xattn_mlp_du_w, L0_xattn_mlp_du_b)
    x = x + _L0_ffn_ref(_layernorm(x, axis=-1), L0_ffn_w1, L0_ffn_mean_w1, L0_ffn_w2, L0_ffn_mean_w2, L0_ffn_w3, L0_ffn_mean_w3)
    return x

_drawn_inputs = setup_inputs


def setup_inputs(seed=0):
    import zlib

    import numpy as np

    out = dict(_drawn_inputs(seed))
    spreads = {'L0_xattn_attn_read_g': (1.0, 0.2),
     'L0_xattn_attn_read_b': (0.0, 0.1),
     'L0_xattn_mlp_read_g': (1.0, 0.2),
     'L0_xattn_mlp_read_b': (0.0, 0.1)}
    factors = {}
    for name, (base, spread) in spreads.items():
        noise = np.random.default_rng([zlib.crc32(name.encode()), seed]).standard_normal(out[name].shape)
        drawn = base * np.exp(spread * noise) if base else spread * noise
        out[name] = jnp.asarray(drawn.astype(out[name].dtype))
    for name, factor in factors.items():
        out[name] = (out[name] * factor).astype(out[name].dtype)
    return out
```

```python
from contextlib import ExitStack

import numpy as np

import concourse.bass as bass
from concourse import mybir

F32 = mybir.dt.float32
F32R = mybir.dt.float32r
BF16 = mybir.dt.bfloat16
I32 = mybir.dt.int32
ALU = mybir.AluOpType
ACT = mybir.ActivationFunctionType
AX = mybir.AxisListType

P = 128
BATCH, SEQ, HID = 2, 512, 1024
H, C, RH = 256, 4, 16
HS = H // RH
DR, M, NH = 8, 1024, 16
HD = H // NH
HALF = HD // 2
INTER = 3584
TILES = BATCH * SEQ // P
TPB = SEQ // P
HH = H // P
KF = HID // P
MT = M // P
JT = INTER // P
BANK = 512
NA = (C - 1) * RH
NAB = 2 * NA + RH
NZ = H + NAB + DR
EPS = 1e-5
SSM_EPS = 1e-5
MASKED = -1e30
GROUP = 2
TWO_PI_BITS = 9


def two_pi_parts():
    left, parts = 2 * np.pi, []
    for _ in range(3):
        step = 2.0 ** (np.floor(np.log2(left)) - (TWO_PI_BITS - 1))
        parts.append(float(np.floor(left / step) * step))
        left -= parts[-1]
    return parts + [float(np.float32(left))]


class Token:

    def __init__(self, sem, step):
        self.sem, self.step, self.used, self.value = sem, step, False, None


class Queue:

    def __init__(self, sem):
        self.sem, self.items = sem, []

    def __call__(self, issue, *after):
        done = Token(self.sem, 1)
        self.items.append((issue, flat(after), done))
        return done

    def dma(self, sem, issue, *after):
        done = Token(sem, 16)
        done.used = True
        self.items.append((issue, flat(after), done))
        return done

    def number(self, values):
        for _, _, done in self.items:
            if done.used:
                values[done.sem] = values.get(done.sem, 0) + done.step
                done.value = values[done.sem]

    def play(self, eng):
        seen = {}
        for issue, after, done in self.items:
            need = {}
            for t in after:
                need[t.sem] = max(need.get(t.sem, 0), t.value)
            for sem, value in need.items():
                if seen.get(sem, 0) < value:
                    eng.wait_ge(sem, value)
                    seen[sem] = value
            ins = issue(eng)
            if done.used:
                ins.then_inc(done.sem, done.step)


def flat(tokens):
    out = []
    for t in tokens:
        if isinstance(t, Token):
            t.used = True
            out.append(t)
        elif t is not None:
            out += flat(t)
    return out


class Slot:

    def __init__(self, ap, sem=None):
        self.ap, self.sem, self.free, self.held = ap, sem, [], False

    def release(self, *tokens):
        self.free, self.held = list(tokens), False


class Ring:

    def __init__(self, slots):
        self.slots = slots

    def take(self):
        while all(s.held for s in self.slots):
            yield
        return self.now()

    def now(self):
        s = next(s for s in self.slots if not s.held)
        s.held = True
        self.slots = [x for x in self.slots if x is not s] + [s]
        return s


def activation(*operands, **options):
    return lambda eng: eng.activation(*operands, **options)


def bn_aggr(*operands, **options):
    return lambda eng: eng.bn_aggr(*operands, **options)


def bn_stats(*operands, **options):
    return lambda eng: eng.bn_stats(*operands, **options)


def dma_start(*operands, **options):
    return lambda eng: eng.dma_start(*operands, **options)


def matmul(*operands, **options):
    return lambda eng: eng.matmul(*operands, **options)


def memset(*operands, **options):
    return lambda eng: eng.memset(*operands, **options)


def reciprocal(*operands, **options):
    return lambda eng: eng.reciprocal(*operands, **options)


def scalar_tensor_tensor(*operands, **options):
    return lambda eng: eng.scalar_tensor_tensor(*operands, **options)


def tensor_copy(*operands, **options):
    return lambda eng: eng.tensor_copy(*operands, **options)


def tensor_reduce(*operands, **options):
    return lambda eng: eng.tensor_reduce(*operands, **options)


def tensor_scalar(*operands, **options):
    return lambda eng: eng.tensor_scalar(*operands, **options)


def tensor_tensor(*operands, **options):
    return lambda eng: eng.tensor_tensor(*operands, **options)


def transpose(*operands, **options):
    return lambda eng: eng.transpose(*operands, **options)


def weave(lanes):
    lanes = list(lanes)
    while lanes:
        for lane in list(lanes):
            try:
                next(lane)
            except StopIteration:
                lanes.remove(lane)


def bass_layer(nc: bass.Bass, d: dict, out: bass.AP):
    with ExitStack() as whole:
        def sem(name):
            return whole.enter_context(nc.semaphore(name))

        def sb(stack, name, shape, dt=F32):
            return stack.enter_context(nc.sbuf_tensor(name, shape, dt))

        pe, act, dve, pool = (Queue(sem(n)) for n in ("s_pe", "s_act", "s_dve", "s_pool"))
        sp = Queue(sem("s_sp"))

        hid = sb(whole, "hid", [P, TILES, HID])
        ident = sb(whole, "ident", [P, P])
        raw_slots, work_slots = [], []
        for n in range(2):
            raw_slots.append(Slot((sb(whole, f"raw_w{n}", [P, HID]), sb(whole, f"raw_b{n}", [P, HID])),
                                  sem(f"s_raw{n}")))
        raws = Ring(raw_slots)
        coeff = sb(whole, "coeff", [P, 3])
        eps = sb(whole, "eps", [P, 1])

        pairs = Ring([Slot(whole.enter_context(nc.psum_tensor(f"pair{n}", [P, 2, BANK], F32)))
                      for n in range(2)])
        banks = [whole.enter_context(nc.psum_tensor(f"bank{n}", [P, BANK], F32)) for n in range(4)]
        singles = Ring([Slot(b) for b in banks[:3]])
        obank = Slot(banks[3])

        e_eps = pool(memset(eps[:, :], EPS))

        names = ("w1", "w3", "w2")

        def load_raw(which, j, slot):
            w, b = slot.ap
            sp.dma(slot.sem, dma_start(w[:, :], d[which][j]), slot.free)
            return sp.dma(slot.sem, dma_start(b[:, :], d["mean_" + which][j]), slot.free)

        attention = whole.enter_context(ExitStack())

        def sba(name, shape, dt=F32):
            return sb(attention, name, shape, dt)

        def load(name, buf, src):
            return sp.dma(sem("s_ld_" + name), dma_start(buf, src))

        l_ident = load("ident", ident[:, :], d["ident"])
        x_loaded = []
        for t in range(TILES):
            x_loaded.append(sp.dma(sem(f"s_x{t}"), dma_start(hid[:, t, :], d["x"][t])))
            if t == 0:
                inw = sba("inw", [P, HH * C * 5])
                l_inw = load("inw", inw[:, :], d["inw"])
                pos_i = sba("pos_i", [P, TILES], I32)
                l_pos = load("pos", pos_i[:, :], d["pos"])
                inv = sba("inv", [P, HALF])
                l_inv = load("inv", inv[:, :], d["inv_freq"])
                gb = sba("gb", [P, HH, 5, 2])
                l_gb = load("gb", gb[:, :, :, :], d["gb"])
                wqkv = sba("wqkv", [P, HH, 3 * H])
                l_wqkv = load("wqkv", wqkv[:, :, :], d["wqkv"])
                cmask = sba("cmask", [P, P])
                l_cmask = load("cmask", cmask[:, :], d["cmask"])
        wcat, l_wcat, bias_ab, l_bias, dut, l_dut, dub, l_dub = [], [], [], [], [], [], [], []
        for n, kt in enumerate((HH, MT)):
            wcat.append(sba(f"wcat{n}", [P, kt, NZ]))
            l_wcat.append(load(f"wcat{n}", wcat[n][:, :, :], d[f"wcat{n}"]))
            bias_ab.append(sba(f"bias_ab{n}", [P, NAB + DR]))
            l_bias.append(load(f"bias_ab{n}", bias_ab[n][:, :], d[f"bias_ab{n}"]))
            dut.append(sba(f"dut{n}", [DR, H]))
            l_dut.append(load(f"dut{n}", dut[n][:, :], d[f"dut{n}"]))
            dub.append(sba(f"dub{n}", [P, H]))
            l_dub.append(load(f"dub{n}", dub[n][:, :], d[f"dub{n}"]))
        ctxw = sba("ctxw", [P, HH, 2, M])
        l_ctx = load("ctx", ctxw[:, :, :, :], d["ctx"])

        big = [sba(f"big{b}", [P, 8, SEQ]) for b in range(BATCH)]
        identb = sba("identb", [P, P], BF16)
        maskb = sba("maskb", [P, P], BF16)
        e_maskb = [dve(tensor_copy(identb[:, :], ident[:, :]), l_ident),
                   dve(tensor_copy(maskb[:, :], cmask[:, :]), l_cmask)]

        diag = [sba("diag0", [P, HH, C, 3, P]), sba("diag1", [P, HH, C, 2, P])]
        e_diag = [[], []]
        for n, (lo, ro) in enumerate(((0, 3), (3, 2))):
            for hh in range(HH):
                for c in range(C):
                    for o in range(ro):
                        col = (hh * C + c) * 5 + lo + o
                        e_diag[n].append((dve if n == 0 else pool)(
                            tensor_scalar(
                                diag[n][:, hh, c, o, :], ident[:, :], inw[:, col:col + 1], None, ALU.mult),
                            l_ident, l_inw))
        e_diag = [x[-1] for x in e_diag]

        rope = sba("rope", [P, 4, TILES, HALF])
        rcos = sba("rcos", [P, TILES, 2, HALF])
        rsin = sba("rsin", [P, TILES, 2, HALF])
        posf = sba("posf", [P, TILES])
        ang, turns, half_sin, whole_sin = (rope[:, n, :, :] for n in range(4))
        magic = float(1.5 * 2 ** 23)
        t = dve(tensor_copy(posf[:, :], pos_i[:, :]), l_pos)
        t = dve(tensor_tensor(ang, posf[:, :].unsqueeze(2).to_broadcast([P, TILES, HALF]),
                                          inv[:, :].unsqueeze(1).to_broadcast([P, TILES, HALF]), ALU.mult), t, l_inv)
        t = dve(tensor_scalar(turns, ang, float(1 / (2 * np.pi)), magic, ALU.mult, ALU.add), t)
        t = dve(tensor_scalar(turns, turns, -magic, None, ALU.add), t)
        for part in two_pi_parts():
            t = dve(scalar_tensor_tensor(ang, turns, -part, ang, ALU.mult, ALU.add), t)
        t = dve(tensor_scalar(ang, ang, 3.1415925, -3.1415925, ALU.min, ALU.max), t)
        t1 = act(activation(whole_sin, ang, ACT.Sin), t)
        t2 = act(activation(half_sin, ang, ACT.Sin, scale=0.5), t)
        t3 = dve(tensor_tensor(half_sin, half_sin, half_sin, ALU.mult), t2)
        e_rope = []
        for n in range(2):
            e_rope.append(dve(tensor_scalar(rcos[:, :, n, :], half_sin, -2.0, 1.0, ALU.mult, ALU.add), t3))
            e_rope.append(dve(tensor_scalar(rsin[:, :, n, :], whole_sin, 2.0 * n - 1.0, None, ALU.mult), t1))

        qkv_bias = sba("qkv_bias", [P, 3 * H])
        ones = sba("ones", [P, P])
        e_ones = pool(memset(ones[:, :], 1.0))
        pq = pairs.now()
        last = None
        for hh in range(HH):
            for o in range(3):
                last = dve(tensor_scalar(big[0][:, hh, o * P:(o + 1) * P], ones[:, :], gb[:, hh, o, 1:2], None, ALU.mult),
                           e_ones, l_gb)
        for o in range(3):
            for hh in range(HH):
                t = pe(matmul(pq.ap[:, o // 2, (o % 2) * H:(o % 2 + 1) * H], big[0][:, hh, o * P:(o + 1) * P],
                                                      wqkv[:, hh, o * H:(o + 1) * H], start=hh == 0, stop=hh == HH - 1),
                       last, l_wqkv, pq.free)
        e_qb = [act(activation(qkv_bias[:, 0:2 * H], pq.ap[:, 0, :], ACT.Copy), t),
                act(activation(qkv_bias[:, 2 * H:], pq.ap[:, 1, 0:H], ACT.Copy), t)]
        pq.release(e_qb)
        e_wqkv = []
        for hh in range(HH):
            for o in range(3):
                e_wqkv.append(pool(tensor_scalar(
                    wqkv[:, hh, o * H:(o + 1) * H], wqkv[:, hh, o * H:(o + 1) * H], gb[:, hh, o, 0:1], None, ALU.mult), t))
        mlp_bias = sba("mlp_bias", [P, 2, MT])
        pq = pairs.now()
        for g in range(2):
            for m in range(MT):
                for hh in range(HH):
                    t = pe(matmul(
                        pq.ap[:, 0, g * MT + m:g * MT + m + 1], ctxw[:, hh, g, m * P:(m + 1) * P],
                        gb[:, hh, 3 + g, 1:2], start=hh == 0, stop=hh == HH - 1), l_ctx, l_gb, pq.free)
        e_mb = act(activation(mlp_bias[:, :, :], pq.ap[:, 0, 0:2 * MT].rearrange("p (g m) -> p g m", g=2), ACT.Copy), t)
        pq.release(e_mb)
        e_ctx = []
        for hh in range(HH):
            for g in range(2):
                e_ctx.append(pool(tensor_scalar(
                    ctxw[:, hh, g, :], ctxw[:, hh, g, :], gb[:, hh, 3 + g, 0:1], None, ALU.mult), t))

        xT = Ring([Slot(sba(f"xT{n}", [P, KF, P]), sem(f"s_xT{n}")) for n in range(2)])
        yT = Ring([Slot(sba(f"yT{n}", [P, 3 * HH, P])) for n in range(3)])
        qk = Ring([Slot(sba("qk", [P, 2 * H]))])
        wideqk = Ring([Slot(sba("wideqk", [P, 2 * NH, 2 * HD]))])
        rot = Ring([Slot(sba(f"rot{n}", [P, 2 * H])) for n in range(1)])
        v = sba("v", [P, TILES, H])
        prob = Ring([Slot(sba(f"prob{n}", [P, BANK])) for n in range(2)])
        probT = Ring([Slot(sba(f"probT{n}", [P, BANK])) for n in range(2)])
        stat = sba("stat", [P, 2, 32])
        negmax = sba("negmax", [P, 2, NH])
        sums = sba("sums", [P, 2, NH])
        o_sb = Ring([Slot(sba("o_sb", [P, H]))])
        inT = [sba("inT", [P, 2 * HH, SEQ])]
        wr = Ring([Slot({k: sba(f"wr_{k}{n}", [P, w]) for k, w in
                         (("z", H + NA), ("e", H + NA), ("b", NAB + DR), ("out", H), ("r", NA),
                          ("a", 3 * H), ("dl", P))}) for n in range(1)])
        e_pad = [pool(memset(s.ap[:, :, :], 0.0)) for s in wideqk.slots]

        stats_free = [[], []]

        def rsqrt_of(var, n, scratch, after):
            lnv, y = scratch[:, 0:n], scratch[:, n:2 * n]
            t = act(activation(lnv, var, ACT.Ln, bias=eps[:, 0:1]), after, e_eps)
            t = act(activation(y, lnv, ACT.Exp, scale=-0.5), t)
            t = dve(tensor_tensor(lnv, y, y, ALU.mult), t)
            t = dve(scalar_tensor_tensor(lnv, var, EPS, lnv, ALU.add, ALU.mult), t)
            t = dve(tensor_scalar(lnv, lnv, -0.5, 1.5, ALU.mult, ALU.add), t)
            return dve(tensor_tensor(y, y, lnv, ALU.mult), t), y

        def layernorm(t, lane, after, target):
            st = stat[:, lane, :]
            a = [dve(bn_stats(st[:, 6 * n:6 * n + 6], hid[:, t, n * BANK:(n + 1) * BANK]),
                     after, stats_free[lane]) for n in range(2)]
            a = dve(bn_aggr(st[:, 12:14], st[:, 0:12]), a)
            a, r = rsqrt_of(st[:, 13:14], 1, st[:, 14:16], a)
            a = dve(tensor_scalar(target, hid[:, t, :], st[:, 12:13], r, ALU.subtract, ALU.mult), a)
            stats_free[lane] = [a]
            return a

        def transposed_tile(src_block, blocks, after, slot, pair, scale=1.0):
            for k in range(blocks):
                a = pe(transpose(pair.ap[:, k // 4, (k % 4) * P:(k % 4 + 1) * P], src_block(k), ident[:, :]),
                       after, pair.free, l_ident)
            return a

        def rat_in(t, lane, n, ways, after):
            pair = yield from pairs.take()
            xt = yield from xT.take()
            a = transposed_tile(lambda k: hid[:, t, k * P:(k + 1) * P], KF, after, xt, pair)
            ev = act(activation(xt.ap[:, :, :].rearrange("p (a b) c -> p a (b c)", a=2), pair.ap[:, :, :], ACT.Copy), a, xt.free)
            pair.release(ev)
            yield
            py = yield from pairs.take()
            for hh in range(HH):
                for c in range(C):
                    a = pe(matmul(py.ap[:, hh, 0:ways * P], xt.ap[:, c * HH + hh, :],
                                                          diag[n][:, hh, c, :, :].rearrange("p o m -> p (o m)"),
                                                          start=c == 0, stop=c == C - 1), ev, e_diag[n], py.free)
            xt.release(a)
            yield
            st = stat[:, lane, :]
            y = yield from yT.take()
            view = py.ap[:, :, 0:ways * P].rearrange("p a (o m) -> p o a m", o=ways)
            for o in range(ways):
                s = dve(bn_stats(st[:, 6 * o:6 * o + 6], view[:, o]), a, stats_free[lane])
                s = dve(bn_aggr(st[:, 18 + 2 * o:20 + 2 * o], st[:, 6 * o:6 * o + 6]), s)
            mv = st[:, 18:24].rearrange("p (o two) -> p o two", two=2)
            s, r = rsqrt_of(mv[:, 0:ways, 1:2].rearrange("p o x -> p (o x)"), ways, st[:, 0:6], s)
            for o in range(ways):
                s = dve(tensor_scalar(y.ap[:, o * HH:(o + 1) * HH, :], view[:, o], st[:, 18 + 2 * o:19 + 2 * o], r[:, o:o + 1],
                                                       ALU.subtract, ALU.mult), s, y.free)
            stats_free[lane] = [s]
            py.release(s)
            yield
            pair = yield from pairs.take()
            a = transposed_tile(lambda k: y.ap[:, k, :], ways * HH, s, None, pair)
            y.release(a)
            return pair, a

        q_ready = [None] * TILES
        big_free = [e_qb, []]

        def front(t, lane):
            b, col = t // TPB, (t % TPB) * P
            ln = layernorm(t, lane, x_loaded[t], hid[:, t, :])
            yield
            pair, a = yield from rat_in(t, lane, 0, 3, ln)
            y = yield from yT.take()
            ev = [act(activation(y.ap[:, 0:4, :], pair.ap[:, 0, :].rearrange("p (a b) -> p a b", a=4), ACT.Copy), a, y.free),
                  act(activation(y.ap[:, 4:6, :], pair.ap[:, 1, 0:2 * P].rearrange("p (a b) -> p a b", a=2), ACT.Copy), a, y.free)]
            pair.release(ev)
            yield
            pair = yield from pairs.take()
            for o in range(3):
                for hh in range(HH):
                    a = pe(matmul(pair.ap[:, o // 2, (o % 2) * H:(o % 2 + 1) * H], y.ap[:, o * HH + hh, :],
                                                          wqkv[:, hh, o * H:(o + 1) * H], start=hh == 0, stop=hh == HH - 1),
                           ev, e_wqkv, pair.free)
            y.release(a)
            yield
            s = yield from qk.take()
            r = yield from rot.take()
            e1 = dve(tensor_tensor(s.ap[:, 0:2 * H], pair.ap[:, 0, :], qkv_bias[:, 0:2 * H], ALU.add), a, s.free, e_qb)
            e2 = dve(tensor_tensor(v[:, t, :], pair.ap[:, 1, 0:H], qkv_bias[:, 2 * H:], ALU.add), a, e_qb)
            pair.release(e1, e2)
            heads = s.ap[:, 0:2 * H].rearrange("p (g two f) -> p g two f", two=2, f=HALF)
            turned = r.ap[:, :].rearrange("p (g two f) -> p g two f", two=2, f=HALF)
            sh = [P, 2 * NH, HALF]
            e3 = [dve(tensor_tensor(turned[:, :, n, :], heads[:, :, 1 - n, :],
                                                     rsin[:, t, n, :].unsqueeze(1).to_broadcast(sh), ALU.mult), e1, r.free, e_rope)
                  for n in range(2)]
            e4 = dve(tensor_tensor(s.ap[:, 0:2 * H].rearrange("p (g f) -> p g f", f=HD),
                                               s.ap[:, 0:2 * H].rearrange("p (g f) -> p g f", f=HD),
                                               rcos[:, t, :, :].rearrange("p a b -> p (a b)").unsqueeze(1).to_broadcast([P, 2 * NH, HD]), ALU.mult), e3)
            wide = yield from wideqk.take()
            e5 = pool(tensor_tensor(wide.ap[:, :, 0:HD], s.ap[:, :].rearrange("p (g f) -> p g f", f=HD),
                                                r.ap[:, :].rearrange("p (g f) -> p g f", f=HD), ALU.add), e4, wide.free, e_pad)
            r.release(e5)
            s.release(e5)
            yield
            pair = yield from pairs.take()
            for k in range(8):
                a = pe(transpose(pair.ap[:, k // 4, (k % 4) * P:(k % 4 + 1) * P],
                                             wide.ap[:, 4 * k:4 * k + 4, :].rearrange("p a b -> p (a b)"), ident[:, :]),
                       e5, pair.free)
            wide.release(a)
            ev = [act(activation(big[b][:, 4 * n:4 * n + 4, col:col + P],
                                                  pair.ap[:, n, :].rearrange("p (a b) -> p a b", a=4), ACT.Copy,
                                                  scale=(0.25, 1.0)[n]), a, big_free[b]) for n in range(2)]
            pair.release(ev)
            q_ready[t] = ev + [e2]

        att_ready = [None] * TILES

        def attend(t):
            b, i = t // TPB, t % TPB
            while any(q_ready[b * TPB + k] is None for k in range(i + 1)):
                yield
            ready = [q_ready[b * TPB + k] for k in range(i + 1)]
            n = (i + 1) * P
            per = max(1, BANK // n)
            par = t % 2
            order = [4 * q + r for r in range(4) for q in range(4)] if per > 1 else list(range(NH))
            groups = [order[g:g + per] for g in range(0, NH, per)]
            held = {}

            def scores(g):
                s = yield from singles.take()
                for u, h in enumerate(groups[g]):
                    row = (h % 4) * 32
                    pe(matmul(
                        s.ap[:, u * n:(u + 1) * n], big[b][row:row + HD, h // 4, i * P:(i + 1) * P],
                        big[b][row:row + HD, 4 + h // 4, 0:n], start=True, stop=False), ready, s.free)
                    a = pe(matmul(s.ap[:, (u + 1) * n - P:(u + 1) * n], identb[:, :], maskb[:, :],
                                                   start=False, stop=True), e_maskb)
                h0 = g * per
                m = dve(tensor_reduce(negmax[:, par, h0:h0 + per], s.ap[:, 0:per * n].rearrange("p (u n) -> p u n", u=per),
                                                  AX.X, ALU.max, negate=True), a)
                p = yield from prob.take()
                for u, h in enumerate(groups[g]):
                    a = act(activation(p.ap[:, u * n:(u + 1) * n], s.ap[:, u * n:(u + 1) * n], ACT.Exp,
                                                             bias=negmax[:, par, h0 + u:h0 + u + 1], accum_out=sums[:, par, h0 + u:h0 + u + 1]), m, p.free)
                s.release(a)
                held[g] = (p, a)

            def turn(g):
                p, a = held[g]
                s = yield from singles.take()
                for k in range(per * (i + 1)):
                    x = pe(transpose(s.ap[:, k * P:(k + 1) * P], p.ap[:, k * P:(k + 1) * P], ident[:, :]), a, s.free)
                p.release(x)
                q = yield from probT.take()
                w = per * n
                if g % 2:
                    x = dve(tensor_copy(q.ap[:, 0:w], s.ap[:, 0:w]), x, q.free)
                else:
                    x = act(activation(q.ap[:, 0:w], s.ap[:, 0:w], ACT.Copy), x, q.free)
                s.release(x)
                held[g] = (q, x)

            def gather(g):
                q, a = held.pop(g)
                for u, h in enumerate(groups[g]):
                    for k in range(i + 1):
                        x = pe(matmul(
                            obank.ap[:, h * HD:(h + 1) * HD], q.ap[:, (u * (i + 1) + k) * P:(u * (i + 1) + k + 1) * P],
                            v[:, b * TPB + k, h * HD:(h + 1) * HD], start=k == 0, stop=k == i), a, ready, obank.free)
                q.release(x)
                return x

            for g in range(len(groups) + 2):
                if g < len(groups):
                    yield from scores(g)
                if 0 <= g - 1 < len(groups):
                    yield from turn(g - 1)
                if 0 <= g - 2 < len(groups):
                    x = gather(g - 2)
                yield
            o = yield from o_sb.take()
            r = dve(reciprocal(sums[:, par, :], sums[:, par, :]), x)
            by_head = sums[:, par, :].rearrange("p (r q) -> p q r" if per > 1 else "p (q r) -> p q r", q=4)
            r = dve(tensor_tensor(o.ap[:, :].rearrange("p (q r f) -> p q r f", q=4, f=HD),
                                              obank.ap[:, 0:H].rearrange("p (q r f) -> p q r f", q=4, f=HD),
                                              by_head.unsqueeze(3).to_broadcast([P, 4, 4, HD]), ALU.mult), r, o.free)
            obank.release(r)
            s = yield from singles.take()
            for hh in range(HH):
                a = pe(transpose(s.ap[:, hh * P:(hh + 1) * P], o.ap[:, hh * P:(hh + 1) * P], ident[:, :]), r, s.free)
            o.release(a)
            y = yield from yT.take()
            a = act(activation(y.ap[:, 0:HH, :], s.ap[:, 0:HH * P].rearrange("p (a b) -> p a b", a=HH), ACT.Copy), a, y.free)
            s.release(a)
            att_ready[t] = (y, a)

        def rat_out(t, n, kt, yblock, after, done_with_y, h_ready):
            pair = yield from pairs.take()
            for k in range(kt):
                a = pe(matmul(pair.ap[:, 0, 0:NZ], yblock(k), wcat[n][:, k, :], start=k == 0, stop=k == kt - 1),
                       after, l_wcat[n], pair.free)
            done_with_y(a)
            w = yield from wr.take()
            z, ez, bb, ov, rr, aa, dl = (w.ap[k] for k in ("z", "e", "b", "out", "r", "a", "dl"))
            f = w.free
            e1 = dve(tensor_tensor(bb[:, :], pair.ap[:, 0, H:NZ], bias_ab[n][:, :], ALU.add), a, f, l_bias[n])
            e2 = act(activation(ov[:, :], pair.ap[:, 0, 0:H], ACT.Copy), a, f, e1)
            a = pe(transpose(pair.ap[0:DR, 1, 0:P], bb[:, NAB:NAB + DR], ident[:, :]), e1)
            a = act(activation(dl[0:DR, :], pair.ap[0:DR, 1, 0:P], ACT.Copy), a, f)
            a = pe(matmul(pair.ap[:, 1, P:P + H], dl[0:DR, :], dut[n][:, :], start=True, stop=True), a, l_dut[n])
            yield
            e3 = dve(tensor_tensor(z[:, 0:H], pair.ap[:, 1, P:P + H], dub[n][:, :], ALU.add), a, f, l_dub[n])
            pair.release(e2, e3)
            e4 = dve(tensor_copy(z[:, H:], bb[:, 0:NA]), e1)
            a = act(activation(ez[:, :], z[:, :], ACT.Abs), e3, e4, f)
            a = act(activation(ez[:, :], ez[:, :], ACT.Exp, scale=-1.0), a)
            a = act(activation(ez[:, :], ez[:, :], ACT.Ln, bias=1.0), a)
            e5 = dve(scalar_tensor_tensor(z[:, :], z[:, :], 0.0, ez[:, :], ALU.max, ALU.add), a)
            delta, nega = z[:, 0:H], z[:, H:]
            wide = [P, C - 1, RH, HS]
            spread = [P, NA, HS]
            e6 = dve(tensor_tensor(aa[:, :].rearrange("p (c g s) -> p c g s", c=C - 1, s=HS),
                                               delta.rearrange("p (g s) -> p g s", s=HS).unsqueeze(1).to_broadcast(wide),
                                               nega.rearrange("p (c g) -> p c g", c=C - 1).unsqueeze(3).to_broadcast(wide), ALU.mult), e5, f)
            e7 = dve(tensor_scalar(rr[:, :], nega, -1.0, -SSM_EPS, ALU.mult, ALU.add), e5, f)
            e7 = dve(reciprocal(rr[:, :], rr[:, :]), e7)
            e7 = dve(tensor_tensor(rr[:, :], rr[:, :], bb[:, NA:2 * NA], ALU.mult), e7)
            e8 = act(activation(aa[:, :], aa[:, :], ACT.Exp, scale=-1.0), e6)
            yield
            ha = hid[:, t, 0:3 * H]
            e9 = pool(tensor_tensor(ha, ha, aa[:, :], ALU.mult), e8, h_ready)
            e10 = dve(scalar_tensor_tensor(aa[:, :].rearrange("p (g s) -> p g s", s=HS),
                                                       aa[:, :].rearrange("p (g s) -> p g s", s=HS), -1.0,
                                                       rr[:, :].unsqueeze(2).to_broadcast(spread), ALU.add, ALU.mult), e9, e7)
            e11 = dve(tensor_tensor(aa[:, :].rearrange("p (c h) -> p c h", c=C - 1),
                                                aa[:, :].rearrange("p (c h) -> p c h", c=C - 1),
                                                ov[:, :].unsqueeze(1).to_broadcast([P, C - 1, H]), ALU.mult), e10, e2)
            e12 = pool(tensor_tensor(ha, ha, aa[:, :], ALU.add), e11)
            skip = bb[:, 2 * NA:NAB]
            g = pool(tensor_tensor(delta.rearrange("p (g s) -> p g s", s=HS), delta.rearrange("p (g s) -> p g s", s=HS),
                                               skip.unsqueeze(2).to_broadcast([P, RH, HS]), ALU.mult), e6)
            g = pool(tensor_tensor(delta, delta, ov[:, :], ALU.mult), g, e2)
            g = pool(tensor_tensor(hid[:, t, 3 * H:], hid[:, t, 3 * H:], delta, ALU.add), g, h_ready)
            w.release(e12, g, e7)
            return [e12, g]

        h2_ready = [None] * TILES
        inT_ready = [None] * TILES
        inT_free = []

        def back(t, lane):
            while att_ready[t] is None:
                yield
            y, a = att_ready[t]
            h2 = yield from rat_out(t, 0, HH, lambda k: y.ap[:, k, :], a, y.release, q_ready[t])
            h2_ready[t] = h2
            yield
            pair, a = yield from rat_in(t, lane, 1, 2, h2)
            col = (t % TPB) * P
            while t >= TPB and not inT_free:
                yield
            ev = act(activation(inT[0][:, :, col:col + P], pair.ap[:, 0, :].rearrange("p (a b) -> p a b", a=4), ACT.Copy),
                     a, inT_free if t >= TPB else [])
            pair.release(ev)
            inT_ready[t] = ev

        mlp_ready = [[], []]

        def mlp(b):
            while any(inT_ready[t] is None for t in range(b * TPB, (b + 1) * TPB)):
                yield
            ready = inT_ready[b * TPB:(b + 1) * TPB]
            for m in range(MT):
                pair = yield from pairs.take()
                for g in range(2):
                    for hh in range(HH):
                        a = pe(matmul(pair.ap[:, g, :], ctxw[:, hh, g, m * P:(m + 1) * P],
                                                                   inT[0][:, g * HH + hh, :], start=hh == 0, stop=hh == HH - 1),
                               ready, e_ctx, pair.free)
                s = yield from prob.take()
                x = act(activation(s.ap[:, :], pair.ap[:, 0, :], ACT.Silu, bias=mlp_bias[:, 0, m:m + 1]), a, s.free, e_mb)
                x = dve(scalar_tensor_tensor(big[b][:, m, :], pair.ap[:, 1, :], mlp_bias[:, 1, m:m + 1], s.ap[:, :],
                                                              ALU.add, ALU.mult), x, [att_ready[t][1] for t in range(b * TPB, (b + 1) * TPB)])
                s.release(x)
                pair.release(x)
            inT_free.append(a)
            mlp_ready[b] = [x]

        x2_ready = [None] * TILES

        def finish(t):
            b, col = t // TPB, (t % TPB) * P
            while not mlp_ready[b]:
                yield
            xr = yield from xT.take()
            l = sp.dma(xr.sem, dma_start(xr.ap[:, :, :].rearrange("p a b -> p (a b)"), d["x"][t]), xr.free)
            h3 = yield from rat_out(t, 1, MT, lambda k: big[b][:, k, col:col + P], mlp_ready[b], lambda a: None, h2_ready[t])
            a = pool(tensor_tensor(hid[:, t, :], hid[:, t, :], xr.ap[:, :, :].rearrange("p a b -> p (a b)"), ALU.add), h3, l)
            xr.release(a)
            x2_ready[t] = a

        absum = sba("absum", [P, 3, JT])
        raw_done = []

        def measure():
            for n, which in enumerate(names):
                for j in range(JT):
                    s = yield from raws.take()
                    l = load_raw(which, j, s)
                    w, bs = s.ap
                    a = pool(tensor_tensor(w[:, :], w[:, :], bs[:, :], ALU.subtract), l)
                    a = act(activation(w[:, :], w[:, :], ACT.Abs, accum_out=absum[:, n, j:j + 1]), a)
                    s.release(a)
                    raw_done.append(a)
                    yield

        def chain(gens):
            for g in gens:
                yield from g
                yield

        def after_rounds(n, gen):
            for _ in range(n):
                yield
            yield from gen

        weave([chain(front(t, 0) for t in range(TILES)),
               chain(attend(t) for t in range(TILES)),
               chain([x for b in range(BATCH) for x in [*(back(t, 1) for t in range(b * TPB, (b + 1) * TPB)), mlp(b)]]),
               chain(finish(t) for t in range(TILES)),
               measure()])

        csum = sba("csum", [P, 3])
        s = singles.now()
        a = dve(tensor_reduce(csum[:, :], absum[:, :, :], AX.X, ALU.add), raw_done[-1])
        a = pe(matmul(s.ap[:, 0:3], ones[:, :], csum[:, :], start=True, stop=True), a, s.free, e_ones)
        e_coeff = dve(tensor_scalar(coeff[:, :], s.ap[:, 0:3], float(1.0 / (INTER * HID)), None, ALU.mult), a)
        s.release(e_coeff)
        over = [e_coeff, x2_ready[TILES - 1], act(activation(eps[:, :], eps[:, :], ACT.Copy), e_coeff, x2_ready)]
        attention.close()

        ffn = whole.enter_context(ExitStack())

        def sbf(name, shape, dt=F32):
            return sb(ffn, name, shape, dt)

        xnT = [sbf(f"xnT_{p}", [P, KF, TILES * P], F32R) for p in ("hi", "lo")]
        w13 = Ring([Slot([sbf(f"w13_{p}{n}", [P, KF, P], F32R) for p in ("hi", "lo")]) for n in range(3)])
        w2 = Ring([Slot([sbf(f"w2_{p}{n}", [P, HID], F32R) for p in ("hi", "lo")]) for n in range(GROUP + 1)])
        ht = [[sbf(f"h_{p}{k}", [P, TILES * P], F32R) for p in ("hi", "lo")] for k in range(GROUP)]
        works = Ring([Slot(sbf(f"work{n}", [P, HID])) for n in range(2)])
        fstat = sbf("fstat", [P, 32])
        sgf = Ring([Slot(sbf(f"sgf{n}", [P, BANK])) for n in range(2)])
        hf = Ring([Slot(sbf(f"hf{n}", [P, BANK])) for n in range(2)])

        xn_ready = []
        stat_free = [over]
        for t in range(TILES):
            st = fstat
            wk = works.now()
            a = [dve(bn_stats(st[:, 6 * n:6 * n + 6], hid[:, t, n * BANK:(n + 1) * BANK]), x2_ready[t], stat_free)
                 for n in range(2)]
            a = dve(bn_aggr(st[:, 12:14], st[:, 0:12]), a)
            a, r = rsqrt_of(st[:, 13:14], 1, st[:, 14:16], a)
            a = dve(tensor_scalar(wk.ap[:, :], hid[:, t, :], st[:, 12:13], r, ALU.subtract, ALU.mult), a, wk.free)
            stat_free = [a]
            pair = pairs.now()
            a = transposed_tile(lambda k, wk=wk: wk.ap[:, k * P:(k + 1) * P], KF, a, None, pair)
            wk.release(a)
            hi = act(activation(xnT[0][:, :, t * P:(t + 1) * P],
                                                 pair.ap[:, :, :].rearrange("p a (b c) -> p (a b) c", b=4), ACT.Copy), a, over)
            lo = dve(tensor_tensor(xnT[1][:, :, t * P:(t + 1) * P],
                                                    pair.ap[:, :, :].rearrange("p a (b c) -> p (a b) c", b=4),
                                                    xnT[0][:, :, t * P:(t + 1) * P].bitcast(F32), ALU.subtract), hi)
            pair.release(lo)
            xn_ready.append(lo)

        def prepare(which, j, target):
            s = raws.now()
            l = load_raw(which, j, s)
            w, bs = s.ap
            n = names.index(which)
            out_ = target.now()
            hi_, lo_ = (x[:, :, :].rearrange("p a b -> p (a b)") if which != "w2" else x[:, :] for x in out_.ap)
            wk = works.now()
            a = pool(tensor_tensor(w[:, :], w[:, :], bs[:, :], ALU.subtract), l)
            a = act(activation(w[:, :], w[:, :], ACT.Sign), a)
            a = dve(scalar_tensor_tensor(wk.ap[:, :], w[:, :], coeff[:, n:n + 1], bs[:, :], ALU.mult, ALU.add), a, e_coeff, wk.free)
            s.release(a)
            a = act(activation(hi_, wk.ap[:, :], ACT.Copy), a, out_.free, over)
            a = dve(tensor_tensor(lo_, wk.ap[:, :], hi_.bitcast(F32), ALU.subtract), a, out_.free)
            wk.release(a)
            return out_, a

        def passes(stat_parts, mov_parts):
            return [(stat_parts[0], mov_parts[0]), (stat_parts[1], mov_parts[0]), (stat_parts[0], mov_parts[1])]

        acc_ready = [x2_ready[t] for t in range(TILES)]
        order = [(w, j) for g in range(0, JT, GROUP) for j in range(g, g + GROUP) for w in ("w1", "w3")]
        prepared = {}
        h_free = [[] for _ in range(GROUP)]
        need = []
        for g in range(0, JT, GROUP):
            for j in range(g, g + GROUP):
                need += [("w1", j), ("w3", j), ("w2", j)]
        todo = iter(need)

        def prepare_next():
            k = next(todo, None)
            if k is not None:
                prepared[k] = prepare(*k, w2 if k[0] == "w2" else w13)

        for _ in range(3):
            prepare_next()
        stores = []
        for g in range(0, JT, GROUP):
            h_ready = {}
            for kk in range(GROUP):
                j = g + kk
                g_pair, u_pair = pairs.now(), pairs.now()
                for which, pair in (("w1", g_pair), ("w3", u_pair)):
                    ws, e_w = prepared.pop((which, j))
                    for b in range(BATCH):
                        for k in range(KF):
                            for n, (ww, xx) in enumerate(passes(ws.ap, xnT)):
                                a = pe(matmul(
                                    pair.ap[:, b, :], ww[:, k, :], xx[:, k, b * SEQ:(b + 1) * SEQ],
                                    start=k == 0 and n == 0, stop=k == KF - 1 and n == 2),
                                    e_w, xn_ready[:(b + 1) * TPB], pair.free)
                        if which == "w1":
                            sgs = sgf.now()
                            x = act(activation(sgs.ap[:, :], pair.ap[:, b, :], ACT.Silu), a, sgs.free)
                            h_ready[b] = (sgs, x)
                        else:
                            sgs, x = h_ready[b]
                            hs = hf.now()
                            x = dve(tensor_tensor(hs.ap[:, :], sgs.ap[:, :], pair.ap[:, b, :], ALU.mult),
                                    a, x, hs.free)
                            sgs.release(x)
                            cols = slice(b * SEQ, (b + 1) * SEQ)
                            y = act(activation(ht[kk][0][:, cols], hs.ap[:, :], ACT.Copy), x, h_free[kk], over)
                            z = dve(tensor_tensor(ht[kk][1][:, cols], hs.ap[:, :], ht[kk][0][:, cols].bitcast(F32), ALU.subtract), y, h_free[kk])
                            hs.release(z)
                            h_ready[(kk, b)] = z
                    if which == "w1":
                        pair.release(h_ready[0][1], h_ready[1][1])
                    else:
                        pair.release(x)
                    ws.release(a)
                    prepare_next()
                prepare_next() if kk + 1 < GROUP or True else None
            slots = [prepared.pop(("w2", g + kk)) for kk in range(GROUP)]
            for t in range(TILES):
                for half in range(2):
                    bank = singles.now()
                    for kk in range(GROUP):
                        for n, (hh_, ww) in enumerate(passes(ht[kk], slots[kk][0].ap)):
                            a = pe(matmul(
                                bank.ap[:, :], hh_[:, t * P:(t + 1) * P], ww[:, half * BANK:(half + 1) * BANK],
                                start=kk == 0 and n == 0, stop=kk == GROUP - 1 and n == 2),
                                slots[kk][1], h_ready[(kk, t // TPB)], bank.free)
                    a2 = dve(tensor_tensor(hid[:, t, half * BANK:(half + 1) * BANK],
                                                                       hid[:, t, half * BANK:(half + 1) * BANK], bank.ap[:, :], ALU.add),
                             a, acc_ready[t])
                    bank.release(a2)
                acc_ready[t] = a2
                if g + GROUP >= JT:
                    stores.append(sp.dma(sem(f"s_out{t}"), dma_start(out[t], hid[:, t, :]), a2))
            for kk in range(GROUP):
                slots[kk][0].release(a)
                h_free[kk] = [a]
        sp_end = flat(stores)

        values = {}
        for q in (sp, pe, act, dve, pool):
            q.number(values)
        block = whole.enter_context(nc.Block())

        @block.sync
        def _(eng):
            sp.play(eng)
            for t in sp_end:
                eng.wait_ge(t.sem, t.value)

        @block.tensor
        def _(eng):
            pe.play(eng)

        @block.scalar
        def _(eng):
            act.play(eng)

        @block.vector
        def _(eng):
            dve.play(eng)

        @block.gpsimd
        def _(eng):
            pool.play(eng)


def _h_order(a, axis):
    a = np.moveaxis(a, axis, 0)
    a = a.reshape(HS, RH, *a.shape[1:]).swapaxes(0, 1).reshape(H, *a.shape[1:])
    return np.moveaxis(a, 0, axis)


def _f_order(a, axis):
    a = np.moveaxis(a, axis, 0)
    a = a.reshape(HS, RH, C, *a.shape[1:]).transpose(2, 1, 0, *range(3, a.ndim + 2)).reshape(HID, *a.shape[1:])
    return np.moveaxis(a, 0, axis)


def _tiles(a):
    return a.reshape(-1, P, *a.shape[1:]).swapaxes(0, 1)


def _device_arrays(x, pos, ctx, rat_in, rat_out, ffn):
    d = {"x": _f_order(x.reshape(TILES * P, HID), 1).reshape(TILES, P, HID), "pos": pos.reshape(TILES, P).T}
    in_w = np.concatenate([_h_order(rat_in["attn_w"], 0), _h_order(rat_in["mlp_w"], 0)], axis=1)
    d["inw"] = _tiles(in_w).transpose(0, 1, 3, 2).reshape(P, -1)
    gamma = np.concatenate([rat_in["attn_g"], rat_in["mlp_g"]]).reshape(5, H)
    beta = np.concatenate([rat_in["attn_b"], rat_in["mlp_b"]]).reshape(5, H)
    gb = np.stack([_h_order(gamma, 1), _h_order(beta, 1)], axis=-1)
    d["gb"] = gb.reshape(5, HH, P, 2).transpose(2, 1, 0, 3)
    d["wqkv"] = _tiles(_h_order(rat_in["qkv"], 2).reshape(3 * H, H).T)
    d["ctx"] = _tiles(_h_order(ctx, 2).transpose(2, 0, 1))
    for n, w in enumerate(rat_out):
        ab, bias = w["wab"], w["wab_b"]
        def by_c(a):
            return a.reshape(RH, C - 1, *a.shape[1:]).swapaxes(0, 1).reshape(a.shape)
        rows = [_h_order(w["wod"][:H], 0), by_c(ab[:NA]), by_c(ab[NA:2 * NA]), ab[2 * NA:], w["wod"][H:]]
        d[f"wcat{n}"] = _tiles(np.concatenate(rows).T)
        row = np.concatenate([by_c(bias[:NA]), by_c(bias[NA:2 * NA]), bias[2 * NA:], np.zeros(DR, bias.dtype)])
        d[f"bias_ab{n}"] = np.tile(row, (P, 1))
        d[f"dut{n}"] = _h_order(w["du"], 0).T
        d[f"dub{n}"] = np.tile(_h_order(w["du_b"], 0), (P, 1))
    for k, w in ffn.items():
        if k.endswith("w2"):
            d[k] = _f_order(w, 0).T.reshape(JT, P, HID)
        else:
            d[k] = _f_order(w, 1).reshape(JT, P, KF, P).transpose(0, 3, 2, 1).reshape(JT, P, HID)
    d["ident"] = np.eye(P, dtype=np.float32)
    q, k = np.arange(P)[:, None], np.arange(P)[None, :]
    d["cmask"] = np.where(k > q, np.float32(MASKED), np.float32(0)).astype(np.float32)
    half = np.arange(HALF, dtype=np.float32) / np.float32(HALF)
    d["inv_freq"] = np.tile((np.float32(1) / np.power(np.float32(10000), half)).astype(np.float32), (P, 1))
    return {k: np.ascontiguousarray(v) for k, v in d.items()}


def kernel(**inputs):
    import concourse.bacc as bacc
    from concourse.bass_utils import run_bass_kernel_spmd

    i = {k: np.asarray(v) for k, v in inputs.items()}
    a = {k[len("L0_xattn_"):]: v for k, v in i.items() if k.startswith("L0_xattn_")}
    d = _device_arrays(
        i["x"], i["pos_BxS"], i["ctx_1024"],
        {"attn_w": a["attn_read_w"], "attn_g": a["attn_read_g"], "attn_b": a["attn_read_b"], "qkv": a["qkv_w"],
         "mlp_w": a["mlp_read_w"], "mlp_g": a["mlp_read_g"], "mlp_b": a["mlp_read_b"]},
        [{"wod": a[f"{n}_wod_w"], "wab": a[f"{n}_wab_w"], "wab_b": a[f"{n}_wab_b"], "du": a[f"{n}_du_w"],
          "du_b": a[f"{n}_du_b"]} for n in ("attn", "mlp")],
        {k[len("L0_ffn_"):]: v for k, v in i.items() if k.startswith("L0_ffn_")})
    nc = bacc.Bacc("TRN2", target_bir_lowering=False, num_devices=1)
    arrays = {f"in_{k}": v for k, v in d.items()}
    aps = {k: nc.dram_tensor(f"in_{k}", v.shape, mybir.dt.from_np(v.dtype), kind="ExternalInput").ap() for k, v in d.items()}
    out = nc.dram_tensor("out", (TILES, P, HID), F32, kind="ExternalOutput").ap()
    bass_layer(nc, aps, out)
    r = run_bass_kernel_spmd(nc, [arrays], core_ids=[0])
    y = np.asarray(r.results[0]["out"]).reshape(BATCH, SEQ, C, RH, HS)
    return np.ascontiguousarray(y.transpose(0, 1, 4, 3, 2)).reshape(BATCH, SEQ, HID)
```

```python
from contextlib import ExitStack

import numpy as np

import concourse.bass as bass
from concourse import mybir

F32 = mybir.dt.float32
F32R = mybir.dt.float32r
BF16 = mybir.dt.bfloat16
I32 = mybir.dt.int32
ALU = mybir.AluOpType
ACT = mybir.ActivationFunctionType
AX = mybir.AxisListType

P = 128
BATCH, SEQ, HID = 2, 512, 1024
H, C, RH = 256, 4, 16
HS = H // RH
DR, M, NH = 8, 1024, 16
HD = H // NH
HALF = HD // 2
INTER = 3584
TILES = BATCH * SEQ // P
TPB = SEQ // P
HH = H // P
KF = HID // P
MT = M // P
JT = INTER // P
BANK = 512
NA = (C - 1) * RH
NAB = 2 * NA + RH
NZ = H + NAB + DR
EPS = 1e-5
SSM_EPS = 1e-5
MASKED = -1e30
GROUP = 2
TWO_PI_BITS = 9
LN_EXP = "natural_log_exp_and_others"


def two_pi_parts():
    left, parts = 2 * np.pi, []
    for _ in range(3):
        step = 2.0 ** (np.floor(np.log2(left)) - (TWO_PI_BITS - 1))
        parts.append(float(np.floor(left / step) * step))
        left -= parts[-1]
    return parts + [float(np.float32(left))]


class Token:

    def __init__(self, sem, step, about):
        self.sem, self.step, self.used, self.value, self.about = sem, step, False, None, about


class Queue:

    def __init__(self, sem, slowness=1.0):
        self.sem, self.items, self.clock, self.slowness = sem, [], 0.0, slowness

    def add(self, op, after, sem, step):
        issue, cost = op
        after = flat(after)
        for t in after:
            t.used = True
        start = max([self.clock] + [t.about for t in after])
        if step == 1:
            self.clock = start + cost * self.slowness
            done = Token(sem, step, self.clock + 60)
        else:
            self.clock = start + cost - 2000
            done = Token(sem, step, start + cost)
            done.used = True
        self.items.append((issue, after, done))
        return done

    def __call__(self, op, *after):
        return self.add(op, after, self.sem, 1)

    def dma(self, sem, op, *after):
        return self.add(op, after, sem, 16)

    def number(self, values):
        for _, _, done in self.items:
            if done.used:
                values[done.sem] = values.get(done.sem, 0) + done.step
                done.value = values[done.sem]

    def play(self, eng):
        seen = {}
        for issue, after, done in self.items:
            need = {}
            for t in after:
                need[t.sem] = max(need.get(t.sem, 0), t.value)
            for sem, value in need.items():
                if seen.get(sem, 0) < value:
                    eng.wait_ge(sem, value)
                    seen[sem] = value
            ins = issue(eng)
            if done.used:
                ins.then_inc(done.sem, done.step)


def flat(tokens):
    out = []
    for t in tokens:
        if isinstance(t, Token):
            out.append(t)
        elif t is not None:
            out += flat(t)
    return out


class Slot:

    def __init__(self, ap, sem=None):
        self.ap, self.sem, self.free, self.held = ap, sem, [], False

    def release(self, *tokens):
        self.free, self.held = list(tokens), False


class Ring:

    def __init__(self, slots):
        self.slots = slots

    def take(self):
        while all(s.held for s in self.slots):
            yield
        return self.now()

    def now(self):
        s = next(s for s in self.slots if not s.held)
        s.held = True
        self.slots = [x for x in self.slots if x is not s] + [s]
        return s


def columns(ap):
    return int(np.prod(ap.shape[1:]))


def matmul(out, lhsT, rhs, **options):
    passes = 4 if rhs.dtype == F32 else 1
    return lambda eng: eng.matmul(out, lhsT, rhs, **options), passes * max(64, columns(out)) / 2.4


def transpose(out, in_, identity):
    return lambda eng: eng.transpose(out, in_, identity), 107


def activation(out, in_, func, **options):
    return lambda eng: eng.activation(out, in_, func, **options), 190 + columns(in_) / 1.2


def elementwise(emit, out, rate=1.0):
    return emit, 70 + columns(out) / 0.96 * rate


def tensor_tensor(out, in0, in1, op):
    return elementwise(lambda eng: eng.tensor_tensor(out, in0, in1, op), out)


def tensor_scalar(out, in0, scalar1, scalar2, *ops):
    return elementwise(lambda eng: eng.tensor_scalar(out, in0, scalar1, scalar2, *ops), out)


def scalar_tensor_tensor(out, in0, scalar, in1, op0, op1):
    return elementwise(lambda eng: eng.scalar_tensor_tensor(out, in0, scalar, in1, op0, op1), out)


def tensor_copy(out, in_):
    return elementwise(lambda eng: eng.tensor_copy(out, in_), out)


def tensor_reduce(out, in_, axis, op, **options):
    return elementwise(lambda eng: eng.tensor_reduce(out, in_, axis, op, **options), in_)


def reciprocal(out, in_):
    return elementwise(lambda eng: eng.reciprocal(out, in_), out)


def bn_stats(out, in_):
    return elementwise(lambda eng: eng.bn_stats(out, in_), in_)


def bn_aggr(out, in_):
    return elementwise(lambda eng: eng.bn_aggr(out, in_), in_)


def memset(out, value):
    return elementwise(lambda eng: eng.memset(out, value), out)


def load_table(name):
    return lambda eng: eng.preload_act_table_set(name), 1300


def dma_start(out, in_):
    return lambda eng: eng.dma_start(out, in_), columns(out) * P * 4 / 350 + 2000


def weave(lanes):
    when = {n: 0.0 for n in range(len(lanes))}
    now = 0.0
    while when:
        n = min(when, key=lambda k: (when[k], k))
        now = max(now, when[n])
        try:
            tokens = next(lanes[n])
        except StopIteration:
            del when[n]
            continue
        if tokens is None:
            when[n] = now + 50.0
        else:
            when[n] = max([t.about for t in flat([tokens])], default=now)


def drained(lane):
    while True:
        try:
            next(lane)
        except StopIteration as end:
            return end.value


def bass_layer(nc: bass.Bass, d: dict, out: bass.AP):
    with ExitStack() as whole:
        def sem(name):
            return whole.enter_context(nc.semaphore(name))

        def sb(stack, name, shape, dt=F32):
            return stack.enter_context(nc.sbuf_tensor(name, shape, dt))

        pe, act, dve = (Queue(sem(n)) for n in ("s_pe", "s_act", "s_dve"))
        pool = Queue(sem("s_pool"), slowness=2.1)
        sp = Queue(sem("s_sp"))

        hid = sb(whole, "hid", [P, TILES, HID])
        ident = sb(whole, "ident", [P, P])
        raw_slots, work_slots = [], []
        for n in range(2):
            raw_slots.append(Slot((sb(whole, f"raw_w{n}", [P, HID]), sb(whole, f"raw_b{n}", [P, HID])),
                                  sem(f"s_raw{n}")))
        raws = Ring(raw_slots)
        coeff = sb(whole, "coeff", [P, 3])
        eps = sb(whole, "eps", [P, 1])

        pairs = Ring([Slot(whole.enter_context(nc.psum_tensor(f"pair{n}", [P, 2, BANK], F32)))
                      for n in range(2)])
        banks = [whole.enter_context(nc.psum_tensor(f"bank{n}", [P, BANK], F32)) for n in range(4)]
        singles = Ring([Slot(b) for b in banks[:3]])
        obank = Slot(banks[3])

        e_eps = pool(memset(eps[:, :], EPS))

        names = ("w1", "w3", "w2")

        def load_raw(which, j, slot):
            w, b = slot.ap
            sp.dma(slot.sem, dma_start(w[:, :], d[which][j]), slot.free)
            return sp.dma(slot.sem, dma_start(b[:, :], d["mean_" + which][j]), slot.free)

        attention = whole.enter_context(ExitStack())

        def sba(name, shape, dt=F32):
            return sb(attention, name, shape, dt)

        def load(name, buf, src):
            return sp.dma(sem("s_ld_" + name), dma_start(buf, src))

        l_ident = load("ident", ident[:, :], d["ident"])
        x_loaded = []
        for t in range(TILES):
            x_loaded.append(sp.dma(sem(f"s_x{t}"), dma_start(hid[:, t, :], d["x"][t])))
            if t == 0:
                inw = sba("inw", [P, HH * C * 5])
                l_inw = load("inw", inw[:, :], d["inw"])
                pos_i = sba("pos_i", [P, TILES], I32)
                l_pos = load("pos", pos_i[:, :], d["pos"])
                inv = sba("inv", [P, HALF])
                l_inv = load("inv", inv[:, :], d["inv_freq"])
                gb = sba("gb", [P, HH, 5, 2])
                l_gb = load("gb", gb[:, :, :, :], d["gb"])
                wqkv = sba("wqkv", [P, HH, 3 * H])
                l_wqkv = load("wqkv", wqkv[:, :, :], d["wqkv"])
                cmask = sba("cmask", [P, P])
                l_cmask = load("cmask", cmask[:, :], d["cmask"])
        wcat, l_wcat, bias_ab, l_bias, dut, l_dut, dub, l_dub = [], [], [], [], [], [], [], []
        for n, kt in enumerate((HH, MT)):
            wcat.append(sba(f"wcat{n}", [P, kt, NZ]))
            l_wcat.append(load(f"wcat{n}", wcat[n][:, :, :], d[f"wcat{n}"]))
            bias_ab.append(sba(f"bias_ab{n}", [P, NAB + DR]))
            l_bias.append(load(f"bias_ab{n}", bias_ab[n][:, :], d[f"bias_ab{n}"]))
            dut.append(sba(f"dut{n}", [DR, H]))
            l_dut.append(load(f"dut{n}", dut[n][:, :], d[f"dut{n}"]))
            dub.append(sba(f"dub{n}", [P, H]))
            l_dub.append(load(f"dub{n}", dub[n][:, :], d[f"dub{n}"]))
        ctxw = sba("ctxw", [P, HH, 2, M])
        l_ctx = load("ctx", ctxw[:, :, :, :], d["ctx"])

        big = [sba(f"big{b}", [P, 8, SEQ]) for b in range(BATCH)]
        identb = sba("identb", [P, P], BF16)
        maskb = sba("maskb", [P, P], BF16)
        e_maskb = [dve(tensor_copy(identb[:, :], ident[:, :]), l_ident),
                   dve(tensor_copy(maskb[:, :], cmask[:, :]), l_cmask)]

        diag = [sba("diag0", [P, HH, C, 3, P]), sba("diag1", [P, HH, C, 2, P])]
        e_diag = [[], []]
        for n, (lo, ro) in enumerate(((0, 3), (3, 2))):
            for hh in range(HH):
                for c in range(C):
                    for o in range(ro):
                        col = (hh * C + c) * 5 + lo + o
                        e_diag[n].append((dve if n == 0 else pool)(
                            tensor_scalar(
                                diag[n][:, hh, c, o, :], ident[:, :], inw[:, col:col + 1], None, ALU.mult),
                            l_ident, l_inw))
        e_diag = [x[-1] for x in e_diag]

        rope = sba("rope", [P, 4, TILES, HALF])
        rcos = sba("rcos", [P, TILES, 2, HALF])
        rsin = sba("rsin", [P, TILES, 2, HALF])
        posf = sba("posf", [P, TILES])
        ang, turns, half_sin, whole_sin = (rope[:, n, :, :] for n in range(4))
        magic = float(1.5 * 2 ** 23)
        t = dve(tensor_copy(posf[:, :], pos_i[:, :]), l_pos)
        t = dve(tensor_tensor(ang, posf[:, :].unsqueeze(2).to_broadcast([P, TILES, HALF]),
                                          inv[:, :].unsqueeze(1).to_broadcast([P, TILES, HALF]), ALU.mult), t, l_inv)
        t = dve(tensor_scalar(turns, ang, float(1 / (2 * np.pi)), magic, ALU.mult, ALU.add), t)
        t = dve(tensor_scalar(turns, turns, -magic, None, ALU.add), t)
        for part in two_pi_parts():
            t = dve(scalar_tensor_tensor(ang, turns, -part, ang, ALU.mult, ALU.add), t)
        t = dve(tensor_scalar(ang, ang, 3.1415925, -3.1415925, ALU.min, ALU.max), t)
        t1 = act(activation(whole_sin, ang, ACT.Sin), t)
        t2 = act(activation(half_sin, ang, ACT.Sin, scale=0.5), t)
        t3 = dve(tensor_tensor(half_sin, half_sin, half_sin, ALU.mult), t2)
        e_rope = []
        for n in range(2):
            e_rope.append(dve(tensor_scalar(rcos[:, :, n, :], half_sin, -2.0, 1.0, ALU.mult, ALU.add), t3))
            e_rope.append(dve(tensor_scalar(rsin[:, :, n, :], whole_sin, 2.0 * n - 1.0, None, ALU.mult), t1))

        qkv_bias = sba("qkv_bias", [P, 3 * H])
        ones = sba("ones", [P, P])
        e_ones = pool(memset(ones[:, :], 1.0))
        pq = pairs.now()
        last = None
        for hh in range(HH):
            for o in range(3):
                last = dve(tensor_scalar(big[0][:, hh, o * P:(o + 1) * P], ones[:, :], gb[:, hh, o, 1:2], None, ALU.mult),
                           e_ones, l_gb)
        for o in range(3):
            for hh in range(HH):
                t = pe(matmul(pq.ap[:, o // 2, (o % 2) * H:(o % 2 + 1) * H], big[0][:, hh, o * P:(o + 1) * P],
                                                      wqkv[:, hh, o * H:(o + 1) * H], start=hh == 0, stop=hh == HH - 1),
                       last, l_wqkv, pq.free)
        e_qb = [act(activation(qkv_bias[:, 0:2 * H], pq.ap[:, 0, :], ACT.Copy), t),
                act(activation(qkv_bias[:, 2 * H:], pq.ap[:, 1, 0:H], ACT.Copy), t)]
        pq.release(e_qb)
        e_wqkv = []
        for hh in range(HH):
            for o in range(3):
                e_wqkv.append(pool(tensor_scalar(
                    wqkv[:, hh, o * H:(o + 1) * H], wqkv[:, hh, o * H:(o + 1) * H], gb[:, hh, o, 0:1], None, ALU.mult), t))
        mlp_bias = sba("mlp_bias", [P, 2, MT])
        pq = pairs.now()
        for g in range(2):
            for m in range(MT):
                for hh in range(HH):
                    t = pe(matmul(
                        pq.ap[:, 0, g * MT + m:g * MT + m + 1], ctxw[:, hh, g, m * P:(m + 1) * P],
                        gb[:, hh, 3 + g, 1:2], start=hh == 0, stop=hh == HH - 1), l_ctx, l_gb, pq.free)
        e_mb = act(activation(mlp_bias[:, :, :], pq.ap[:, 0, 0:2 * MT].rearrange("p (g m) -> p g m", g=2), ACT.Copy), t)
        pq.release(e_mb)
        e_ctx = []
        for hh in range(HH):
            for g in range(2):
                e_ctx.append(pool(tensor_scalar(
                    ctxw[:, hh, g, :], ctxw[:, hh, g, :], gb[:, hh, 3 + g, 0:1], None, ALU.mult), t))

        xT = Ring([Slot(sba(f"xT{n}", [P, KF, P]), sem(f"s_xT{n}")) for n in range(2)])
        yT = Ring([Slot(sba(f"yT{n}", [P, 3 * HH, P])) for n in range(3)])
        qk = Ring([Slot((sba("qk", [P, 2 * H]), sba("crossed", [P, 2 * H]), sba("wideqk", [P, 2 * NH, 2 * HD])))])
        v = sba("v", [P, TILES, H])
        prob = Ring([Slot(sba(f"prob{n}", [P, BANK])) for n in range(2)])
        probT = Ring([Slot(sba(f"probT{n}", [P, BANK])) for n in range(2)])
        stats = Ring([Slot(sba(f"stat{n}", [P, 24])) for n in range(4)])
        negmax = sba("negmax", [P, 2, NH])
        sums = sba("sums", [P, 2, NH])
        o_sb = Ring([Slot(sba("o_sb", [P, H]))])
        inT = [sba("inT", [P, 2 * HH, SEQ])]
        wr = Ring([Slot({k: sba(f"wr_{k}{n}", [P, w]) for k, w in
                         (("z", H + NA), ("e", H + NA), ("b", NAB + DR), ("out", H), ("r", NA),
                          ("a", 3 * H), ("dl", P))}) for n in range(1)])
        e_pad = [pool(memset(s.ap[2][:, :, :], 0.0)) for s in qk.slots]

        def rsqrt_of(var, n, scratch, after):
            lnv, y = scratch[:, 0:n], scratch[:, n:2 * n]
            t = act(activation(lnv, var, ACT.Ln, bias=eps[:, 0:1]), after, e_eps)
            t = act(activation(y, lnv, ACT.Exp, scale=-0.5), t)
            yield t
            t = dve(tensor_tensor(lnv, y, y, ALU.mult), t)
            t = dve(scalar_tensor_tensor(lnv, var, EPS, lnv, ALU.add, ALU.mult), t)
            t = dve(tensor_scalar(lnv, lnv, -0.5, 1.5, ALU.mult, ALU.add), t)
            return dve(tensor_tensor(y, y, lnv, ALU.mult), t), y

        def layernorm(t, target, after):
            slot = yield from stats.take()
            st = slot.ap
            a = [dve(bn_stats(st[:, 6 * n:6 * n + 6], hid[:, t, n * BANK:(n + 1) * BANK]), after, slot.free) for n in range(2)]
            a = dve(bn_aggr(st[:, 12:14], st[:, 0:12]), a)
            yield a
            a, r = yield from rsqrt_of(st[:, 13:14], 1, st[:, 14:16], a)
            a = dve(tensor_scalar(target, hid[:, t, :], st[:, 12:13], r, ALU.subtract, ALU.mult), a)
            slot.release(a)
            return a

        def turn_blocks(source, blocks, pair, after):
            for k in range(blocks):
                a = pe(transpose(pair.ap[:, k // 4, (k % 4) * P:(k % 4 + 1) * P], source[:, k, :], ident[:, :]), after, pair.free, l_ident)
            return a

        def rat_in(t, n, ways, after):
            xt = yield from xT.take()
            y = yield from yT.take()
            pair = yield from pairs.take()
            a = turn_blocks(hid[:, t, :].rearrange("p (k f) -> p k f", f=P), KF, pair, after)
            yield a
            ev = act(activation(xt.ap[:, :, :].rearrange("p (a b) c -> p a (b c)", a=2), pair.ap[:, :, :], ACT.Copy), a, xt.free)
            pair.release(ev)
            yield ev
            py = yield from pairs.take()
            for hh in range(HH):
                for c in range(C):
                    a = pe(matmul(py.ap[:, hh, 0:ways * P], xt.ap[:, c * HH + hh, :],
                                  diag[n][:, hh, c, :, :].rearrange("p o m -> p (o m)"), start=c == 0, stop=c == C - 1),
                           ev, e_diag[n], py.free)
            xt.release(a)
            yield a
            slot = yield from stats.take()
            st = slot.ap
            view = py.ap[:, :, 0:ways * P].rearrange("p a (o m) -> p o a m", o=ways)
            s = [dve(bn_stats(st[:, 6 * o:6 * o + 6], view[:, o]), a, slot.free) for o in range(ways)]
            s = [dve(bn_aggr(st[:, 18 + 2 * o:20 + 2 * o], st[:, 6 * o:6 * o + 6]), s) for o in range(ways)]
            yield s
            mv = st[:, 18:24].rearrange("p (o two) -> p o two", two=2)
            s, r = yield from rsqrt_of(mv[:, 0:ways, 1:2].rearrange("p o x -> p (o x)"), ways, st[:, 0:6], s)
            s = [dve(tensor_scalar(y.ap[:, o * HH:(o + 1) * HH, :], view[:, o], st[:, 18 + 2 * o:19 + 2 * o], r[:, o:o + 1],
                                   ALU.subtract, ALU.mult), s, y.free) for o in range(ways)]
            slot.release(s)
            py.release(s)
            yield s
            pair = yield from pairs.take()
            a = turn_blocks(y.ap, ways * HH, pair, s)
            yield a
            return y, pair, a

        q_ready = [None] * TILES

        def front(t):
            b, col = t // TPB, (t % TPB) * P
            yield x_loaded[t]
            ln = yield from layernorm(t, hid[:, t, :], x_loaded[t])
            yield ln
            y, pair, a = yield from rat_in(t, 0, 3, ln)
            ev = [act(activation(y.ap[:, 0:4, :], pair.ap[:, 0, :].rearrange("p (a b) -> p a b", a=4), ACT.Copy), a),
                  act(activation(y.ap[:, 4:6, :], pair.ap[:, 1, 0:2 * P].rearrange("p (a b) -> p a b", a=2), ACT.Copy), a)]
            pair.release(ev)
            yield ev
            s = yield from qk.take()
            pair = yield from pairs.take()
            for o in range(3):
                for hh in range(HH):
                    a = pe(matmul(pair.ap[:, o // 2, (o % 2) * H:(o % 2 + 1) * H], y.ap[:, o * HH + hh, :],
                                  wqkv[:, hh, o * H:(o + 1) * H], start=hh == 0, stop=hh == HH - 1),
                           ev, e_wqkv, pair.free)
            y.release(a)
            yield a
            plain, turned, wide = s.ap
            e1 = dve(tensor_tensor(plain[:, :], pair.ap[:, 0, :], qkv_bias[:, 0:2 * H], ALU.add), a, s.free, e_qb)
            e2 = dve(tensor_tensor(v[:, t, :], pair.ap[:, 1, 0:H], qkv_bias[:, 2 * H:], ALU.add), a, e_qb)
            pair.release(e1, e2)
            yield e1
            halves = plain[:, :].rearrange("p (g two f) -> p g two f", two=2, f=HALF)
            crossed = turned[:, :].rearrange("p (g two f) -> p g two f", two=2, f=HALF)
            by_head = plain[:, :].rearrange("p (g f) -> p g f", f=HD)
            e3 = [dve(tensor_tensor(crossed[:, :, n, :], halves[:, :, 1 - n, :],
                                    rsin[:, t, n, :].unsqueeze(1).to_broadcast([P, 2 * NH, HALF]), ALU.mult), e1, e_rope)
                  for n in range(2)]
            e4 = dve(tensor_tensor(by_head, by_head, rcos[:, t, :, :].rearrange("p a b -> p (a b)").unsqueeze(1).to_broadcast([P, 2 * NH, HD]),
                                   ALU.mult), e3)
            yield e4
            e5 = dve(tensor_tensor(wide[:, :, 0:HD], by_head, turned[:, :].rearrange("p (g f) -> p g f", f=HD), ALU.add), e4, e_pad)
            yield e5
            pair = yield from pairs.take()
            a = turn_blocks(wide[:, :, :].rearrange("p (k a) b -> p k (a b)", a=4), 8, pair, e5)
            s.release(a)
            yield a
            ev = [act(activation(big[b][:, 4 * n:4 * n + 4, col:col + P], pair.ap[:, n, :].rearrange("p (a b) -> p a b", a=4), ACT.Copy,
                                 scale=(HD ** -0.5, 1.0)[n]), a, e_qb) for n in range(2)]
            pair.release(ev)
            q_ready[t] = ev + [e2]

        att_ready = [None] * TILES

        def attend(t):
            b, i = t // TPB, t % TPB
            while any(q_ready[b * TPB + k] is None for k in range(i + 1)):
                yield None
            ready = [q_ready[b * TPB + k] for k in range(i + 1)]
            yield ready
            n = (i + 1) * P
            per = max(1, BANK // n)
            par = t % 2
            order = [4 * q + r for r in range(4) for q in range(4)] if per > 1 else list(range(NH))
            groups = [order[g:g + per] for g in range(0, NH, per)]
            held = {}

            def scores(g):
                s = yield from singles.take()
                for u, h in enumerate(groups[g]):
                    row = (h % 4) * 32
                    pe(matmul(s.ap[:, u * n:(u + 1) * n], big[b][row:row + HD, h // 4, i * P:(i + 1) * P],
                              big[b][row:row + HD, 4 + h // 4, 0:n], start=True, stop=False), ready, s.free)
                    a = pe(matmul(s.ap[:, (u + 1) * n - P:(u + 1) * n], identb[:, :], maskb[:, :], start=False, stop=True), e_maskb)
                held[g] = (s, a)

            def soften(g):
                s, a = held[g]
                h0 = g * per
                m = dve(tensor_reduce(negmax[:, par, h0:h0 + per], s.ap[:, 0:per * n].rearrange("p (u n) -> p u n", u=per),
                                      AX.X, ALU.max, negate=True), a)
                p = yield from prob.take()
                for u, h in enumerate(groups[g]):
                    a = act(activation(p.ap[:, u * n:(u + 1) * n], s.ap[:, u * n:(u + 1) * n], ACT.Exp,
                                       bias=negmax[:, par, h0 + u:h0 + u + 1], accum_out=sums[:, par, h0 + u:h0 + u + 1]), m, p.free)
                s.release(a)
                held[g] = (p, a)

            def turn(g):
                p, a = held[g]
                s = yield from singles.take()
                for k in range(per * (i + 1)):
                    x = pe(transpose(s.ap[:, k * P:(k + 1) * P], p.ap[:, k * P:(k + 1) * P], ident[:, :]), a, s.free)
                p.release(x)
                q = yield from probT.take()
                w = per * n
                if g % 2:
                    x = dve(tensor_copy(q.ap[:, 0:w], s.ap[:, 0:w]), x, q.free)
                else:
                    x = act(activation(q.ap[:, 0:w], s.ap[:, 0:w], ACT.Copy), x, q.free)
                s.release(x)
                held[g] = (q, x)

            def gather(g):
                q, a = held.pop(g)
                for u, h in enumerate(groups[g]):
                    for k in range(i + 1):
                        x = pe(matmul(obank.ap[:, h * HD:(h + 1) * HD], q.ap[:, (u * (i + 1) + k) * P:(u * (i + 1) + k + 1) * P],
                                      v[:, b * TPB + k, h * HD:(h + 1) * HD], start=k == 0, stop=k == i), a, ready, obank.free)
                q.release(x)
                return x

            last = len(groups)
            for g in range(last + 2):
                if g < last:
                    yield from scores(g)
                    yield held[g][1]
                if 0 <= g - 2 < last:
                    x = gather(g - 2)
                if g < last:
                    yield from soften(g)
                if 0 <= g - 1 < last:
                    yield held[g - 1][1]
                    yield from turn(g - 1)
            yield x
            o = yield from o_sb.take()
            r = dve(reciprocal(sums[:, par, :], sums[:, par, :]), x)
            by_head = sums[:, par, :].rearrange("p (r q) -> p q r" if per > 1 else "p (q r) -> p q r", q=4)
            r = dve(tensor_tensor(o.ap[:, :].rearrange("p (q r f) -> p q r f", q=4, f=HD),
                                  obank.ap[:, 0:H].rearrange("p (q r f) -> p q r f", q=4, f=HD),
                                  by_head.unsqueeze(3).to_broadcast([P, 4, 4, HD]), ALU.mult), r, o.free)
            obank.release(r)
            yield r
            y = yield from yT.take()
            s = yield from singles.take()
            for hh in range(HH):
                a = pe(transpose(s.ap[:, hh * P:(hh + 1) * P], o.ap[:, hh * P:(hh + 1) * P], ident[:, :]), r, s.free)
            o.release(a)
            yield a
            a = act(activation(y.ap[:, 0:HH, :], s.ap[:, 0:HH * P].rearrange("p (a b) -> p a b", a=HH), ACT.Copy), a, y.free)
            s.release(a)
            att_ready[t] = (y, a)

        def rat_out(t, n, kt, blocks, after, done_with, h_ready):
            pair = yield from pairs.take()
            for k in range(kt):
                a = pe(matmul(pair.ap[:, 0, 0:NZ], blocks[:, k, :], wcat[n][:, k, :], start=k == 0, stop=k == kt - 1),
                       after, l_wcat[n], pair.free)
            if done_with is not None:
                done_with.release(a)
            yield a
            w = yield from wr.take()
            z, ez, bb, ov, rr, aa, dl = (w.ap[k] for k in ("z", "e", "b", "out", "r", "a", "dl"))
            f = w.free
            e1 = dve(tensor_tensor(bb[:, :], pair.ap[:, 0, H:NZ], bias_ab[n][:, :], ALU.add), a, f, l_bias[n])
            e2 = act(activation(ov[:, :], pair.ap[:, 0, 0:H], ACT.Copy), a, f, e1)
            yield e1
            a = pe(transpose(pair.ap[0:DR, 1, 0:P], bb[:, NAB:NAB + DR], ident[:, :]), e1)
            yield a
            a = act(activation(dl[0:DR, :], pair.ap[0:DR, 1, 0:P], ACT.Copy), a, f)
            yield a
            a = pe(matmul(pair.ap[:, 1, P:P + H], dl[0:DR, :], dut[n][:, :], start=True, stop=True), a, l_dut[n])
            yield a
            e3 = dve(tensor_tensor(z[:, 0:H], pair.ap[:, 1, P:P + H], dub[n][:, :], ALU.add), a, f, l_dub[n])
            pair.release(e2, e3)
            e4 = dve(tensor_copy(z[:, H:], bb[:, 0:NA]), e1)
            yield e4
            a = act(activation(ez[:, :], z[:, :], ACT.Abs), e3, e4, f)
            a = act(activation(ez[:, :], ez[:, :], ACT.Exp, scale=-1.0), a)
            a = act(activation(ez[:, :], ez[:, :], ACT.Ln, bias=1.0), a)
            yield a
            e5 = dve(scalar_tensor_tensor(z[:, :], z[:, :], 0.0, ez[:, :], ALU.max, ALU.add), a)
            delta, nega = z[:, 0:H], z[:, H:]
            wide = [P, C - 1, RH, HS]
            e6 = dve(tensor_tensor(aa[:, :].rearrange("p (c g s) -> p c g s", c=C - 1, s=HS),
                                   delta.rearrange("p (g s) -> p g s", s=HS).unsqueeze(1).to_broadcast(wide),
                                   nega.rearrange("p (c g) -> p c g", c=C - 1).unsqueeze(3).to_broadcast(wide), ALU.mult), e5, f)
            e7 = dve(tensor_scalar(rr[:, :], nega, -1.0, -SSM_EPS, ALU.mult, ALU.add), e5, f)
            e7 = dve(reciprocal(rr[:, :], rr[:, :]), e7)
            e7 = dve(tensor_tensor(rr[:, :], rr[:, :], bb[:, NA:2 * NA], ALU.mult), e7)
            yield e6
            e8 = act(activation(aa[:, :], aa[:, :], ACT.Exp, scale=-1.0), e6)
            skip = bb[:, 2 * NA:NAB]
            g = pool(tensor_tensor(delta.rearrange("p (g s) -> p g s", s=HS), delta.rearrange("p (g s) -> p g s", s=HS),
                                   skip.unsqueeze(2).to_broadcast([P, RH, HS]), ALU.mult), e6)
            g = pool(tensor_tensor(delta, delta, ov[:, :], ALU.mult), g, e2)
            g = pool(tensor_tensor(hid[:, t, 3 * H:], hid[:, t, 3 * H:], delta, ALU.add), g, h_ready)
            yield e8
            ha = hid[:, t, 0:3 * H]
            e9 = pool(tensor_tensor(ha, ha, aa[:, :], ALU.mult), e8, h_ready)
            yield e9
            groups = aa[:, :].rearrange("p (g s) -> p g s", s=HS)
            e10 = dve(scalar_tensor_tensor(groups, groups, -1.0, rr[:, :].unsqueeze(2).to_broadcast([P, NA, HS]),
                                           ALU.add, ALU.mult), e9, e7)
            by_c = aa[:, :].rearrange("p (c h) -> p c h", c=C - 1)
            e11 = dve(tensor_tensor(by_c, by_c, ov[:, :].unsqueeze(1).to_broadcast([P, C - 1, H]), ALU.mult), e10, e2)
            e12 = dve(tensor_tensor(ha, ha, aa[:, :], ALU.add), e11)
            w.release(e12, g, e7)
            return [e12, g]

        h2_ready = [None] * TILES
        inT_ready = [None] * TILES
        inT_free = []

        def back(t):
            while att_ready[t] is None:
                yield None
            y, a = att_ready[t]
            yield a
            h2 = yield from rat_out(t, 0, HH, y.ap, a, y, q_ready[t])
            h2_ready[t] = h2
            yield h2
            y, pair, a = yield from rat_in(t, 1, 2, h2)
            y.release(a)
            col = (t % TPB) * P
            while t >= TPB and not inT_free:
                yield None
            ev = act(activation(inT[0][:, :, col:col + P], pair.ap[:, 0, :].rearrange("p (a b) -> p a b", a=4), ACT.Copy),
                     a, inT_free if t >= TPB else [])
            pair.release(ev)
            inT_ready[t] = ev

        mlp_ready = [[], []]

        def mlp(b):
            while any(inT_ready[t] is None for t in range(b * TPB, (b + 1) * TPB)):
                yield None
            ready = inT_ready[b * TPB:(b + 1) * TPB]
            yield ready
            for m in range(MT):
                pair = yield from pairs.take()
                s = yield from prob.take()
                for g in range(2):
                    for hh in range(HH):
                        a = pe(matmul(pair.ap[:, g, :], ctxw[:, hh, g, m * P:(m + 1) * P], inT[0][:, g * HH + hh, :],
                                      start=hh == 0, stop=hh == HH - 1), ready, e_ctx, pair.free)
                x = act(activation(s.ap[:, :], pair.ap[:, 0, :], ACT.Silu, bias=mlp_bias[:, 0, m:m + 1]), a, s.free, e_mb)
                x = dve(scalar_tensor_tensor(big[b][:, m, :], pair.ap[:, 1, :], mlp_bias[:, 1, m:m + 1], s.ap[:, :],
                                             ALU.add, ALU.mult), x, [att_ready[t][1] for t in range(b * TPB, (b + 1) * TPB)])
                s.release(x)
                pair.release(x)
            act(load_table(LN_EXP))
            inT_free.append(a)
            mlp_ready[b] = [x]

        x2_ready = [None] * TILES

        def finish(t):
            b, col = t // TPB, (t % TPB) * P
            while not mlp_ready[b]:
                yield None
            yield mlp_ready[b]
            xr = yield from xT.take()
            again = xr.ap[:, :, :].rearrange("p a b -> p (a b)")
            l = sp.dma(xr.sem, dma_start(again, d["x"][t]), xr.free)
            h3 = yield from rat_out(t, 1, MT, big[b][:, :, col:col + P], mlp_ready[b], None, h2_ready[t])
            yield h3
            a = pool(tensor_tensor(hid[:, t, :], hid[:, t, :], again, ALU.add), h3, l)
            xr.release(a)
            x2_ready[t] = a

        absum = sba("absum", [P, 3, JT])
        raw_done = []

        def measure():
            loads = []
            every = [(n, j) for n in range(3) for j in range(JT)]
            for k in range(len(every) + 2):
                if k >= 2:
                    n, j = every[k - 2]
                    s, l = loads[k - 2]
                    w, bs = s.ap
                    yield l
                    a = (dve if k % 3 == 0 else pool)(tensor_tensor(w[:, :], w[:, :], bs[:, :], ALU.subtract), l)
                    yield a
                    a = act(activation(w[:, :], w[:, :], ACT.Abs, accum_out=absum[:, n, j:j + 1]), a)
                    s.release(a)
                    raw_done.append(a)
                if k < len(every):
                    s = yield from raws.take()
                    loads.append((s, load_raw(names[every[k][0]], every[k][1], s)))

        def chain(gens):
            for g in gens:
                yield from g

        act(load_table(LN_EXP))
        tiles = range(TILES)
        weave([chain(front(t) for t in tiles[0::2]), chain(front(t) for t in tiles[1::2]),
               chain(attend(t) for t in tiles),
               chain(back(t) for t in tiles[0::2]), chain(back(t) for t in tiles[1::2]),
               chain(mlp(b) for b in range(BATCH)),
               chain(finish(t) for t in tiles[0::2]), chain(finish(t) for t in tiles[1::2]),
               measure()])

        csum = sba("csum", [P, 3])
        s = singles.now()
        a = dve(tensor_reduce(csum[:, :], absum[:, :, :], AX.X, ALU.add), raw_done[-1])
        a = pe(matmul(s.ap[:, 0:3], ones[:, :], csum[:, :], start=True, stop=True), a, s.free, e_ones)
        e_coeff = dve(tensor_scalar(coeff[:, :], s.ap[:, 0:3], float(1.0 / (INTER * HID)), None, ALU.mult), a)
        s.release(e_coeff)
        over = [e_coeff, x2_ready[TILES - 1], act(activation(eps[:, :], eps[:, :], ACT.Copy), e_coeff, x2_ready)]
        attention.close()

        ffn = whole.enter_context(ExitStack())

        def sbf(name, shape, dt=F32):
            return sb(ffn, name, shape, dt)

        xnT = [sbf(f"xnT_{p}", [P, KF, TILES * P], F32R) for p in ("hi", "lo")]
        w13 = Ring([Slot([sbf(f"w13_{p}{n}", [P, KF, P], F32R) for p in ("hi", "lo")]) for n in range(3)])
        w2 = Ring([Slot([sbf(f"w2_{p}{n}", [P, HID], F32R) for p in ("hi", "lo")]) for n in range(GROUP + 1)])
        ht = [[sbf(f"h_{p}{k}", [P, TILES * P], F32R) for p in ("hi", "lo")] for k in range(GROUP)]
        works = Ring([Slot(sbf(f"work{n}", [P, HID])) for n in range(2)])
        fstat = Ring([Slot(sbf(f"fstat{n}", [P, 24])) for n in range(2)])
        more = [Slot((sbf(f"raw_wf{n}", [P, HID]), sbf(f"raw_bf{n}", [P, HID])), sem(f"s_rawf{n}")) for n in range(1)]
        for s in more:
            s.release(over)
        raws.slots += more
        raw_slots_f = raws.slots
        sgf = Ring([Slot(sbf(f"sgf{n}", [P, BANK])) for n in range(2)])
        hf = Ring([Slot(sbf(f"hf{n}", [P, BANK])) for n in range(2)])

        xn_ready = [None] * TILES

        def normalise(t):
            yield x2_ready[t]
            wk = yield from works.take()
            st = fstat.now()
            a = [dve(bn_stats(st.ap[:, 6 * n:6 * n + 6], hid[:, t, n * BANK:(n + 1) * BANK]), x2_ready[t], st.free, over)
                 for n in range(2)]
            a = dve(bn_aggr(st.ap[:, 12:14], st.ap[:, 0:12]), a)
            yield a
            a, r = yield from rsqrt_of(st.ap[:, 13:14], 1, st.ap[:, 14:16], a)
            a = dve(tensor_scalar(wk.ap[:, :], hid[:, t, :], st.ap[:, 12:13], r, ALU.subtract, ALU.mult), a, wk.free)
            st.release(a)
            yield a
            pair = yield from pairs.take()
            a = turn_blocks(wk.ap[:, :].rearrange("p (k f) -> p k f", f=P), KF, pair, a)
            wk.release(a)
            yield a
            turned = pair.ap[:, :, :].rearrange("p a (b c) -> p (a b) c", b=4)
            hi = act(activation(xnT[0][:, :, t * P:(t + 1) * P], turned, ACT.Copy), a, over)
            yield hi
            lo = dve(tensor_tensor(xnT[1][:, :, t * P:(t + 1) * P], turned,
                                   xnT[0][:, :, t * P:(t + 1) * P].bitcast(F32), ALU.subtract), hi)
            pair.release(lo)
            xn_ready[t] = lo

        need = [(which, j) for j in range(JT) for which in names]
        todo = iter(need)
        prepared = {}

        def prepare():
            for which, j in todo:
                s = yield from raws.take()
                l = load_raw(which, j, s)
                yield l
                w, bs = s.ap
                n = names.index(which)
                a = pool(tensor_tensor(w[:, :], w[:, :], bs[:, :], ALU.subtract), l)
                yield a
                a = act(activation(w[:, :], w[:, :], ACT.Sign), a)
                yield a
                a = dve(scalar_tensor_tensor(w[:, :], w[:, :], coeff[:, n:n + 1], bs[:, :], ALU.mult, ALU.add), a, e_coeff)
                yield a
                target = yield from (w2 if which == "w2" else w13).take()
                hi_, lo_ = (x[:, :, :].rearrange("p a b -> p (a b)") if which != "w2" else x[:, :] for x in target.ap)
                a = act(activation(hi_, w[:, :], ACT.Copy), a, target.free, over)
                yield a
                a = dve(tensor_tensor(lo_, w[:, :], hi_.bitcast(F32), ALU.subtract), a, target.free)
                s.release(a)
                prepared[(which, j)] = (target, a)

        def prepared_tile(key):
            while key not in prepared:
                yield None
            return prepared.pop(key)

        def passes(stat_parts, mov_parts):
            return [(stat_parts[0], mov_parts[0]), (stat_parts[1], mov_parts[0]), (stat_parts[0], mov_parts[1])]

        acc_ready = [x2_ready[t] for t in range(TILES)]
        h_free = [[] for _ in range(GROUP)]
        stores = []

        def products():
            for g in range(0, JT, GROUP):
                h_ready, gated = {}, {}
                for kk in range(GROUP):
                    j = g + kk
                    for which in ("w1", "w3"):
                        ws, e_w = yield from prepared_tile((which, j))
                        pair = yield from pairs.take()
                        for b in range(BATCH):
                            while None in xn_ready[:(b + 1) * TPB]:
                                yield None
                            for k in range(KF):
                                for n, (ww, xx) in enumerate(passes(ws.ap, xnT)):
                                    a = pe(matmul(
                                        pair.ap[:, b, :], ww[:, k, :], xx[:, k, b * SEQ:(b + 1) * SEQ],
                                        start=k == 0 and n == 0, stop=k == KF - 1 and n == 2),
                                        e_w, xn_ready[:(b + 1) * TPB], pair.free)
                            if b == BATCH - 1:
                                ws.release(a)
                            yield a
                            if which == "w1":
                                sg = sgf.now()
                                x = act(activation(sg.ap[:, :], pair.ap[:, b, :], ACT.Silu), a, sg.free)
                                gated[b] = (sg, x)
                            else:
                                sg, x = gated[b]
                                hs = hf.now()
                                x = dve(tensor_tensor(hs.ap[:, :], sg.ap[:, :], pair.ap[:, b, :], ALU.mult), a, x, hs.free)
                                sg.release(x)
                                yield x
                                cols = slice(b * SEQ, (b + 1) * SEQ)
                                y = act(activation(ht[kk][0][:, cols], hs.ap[:, :], ACT.Copy), x, h_free[kk], over)
                                yield y
                                z = dve(tensor_tensor(ht[kk][1][:, cols], hs.ap[:, :], ht[kk][0][:, cols].bitcast(F32),
                                                      ALU.subtract), y, h_free[kk])
                                hs.release(z)
                                h_ready[(kk, b)] = z
                        pair.release(x, gated[0][1])
                tiles2 = []
                for kk in range(GROUP):
                    tiles2.append((yield from prepared_tile(("w2", g + kk))))
                for t in range(TILES):
                    for half in range(2):
                        bank = yield from singles.take()
                        for kk in range(GROUP):
                            for n, (hh_, ww) in enumerate(passes(ht[kk], tiles2[kk][0].ap)):
                                a = pe(matmul(
                                    bank.ap[:, :], hh_[:, t * P:(t + 1) * P], ww[:, half * BANK:(half + 1) * BANK],
                                    start=kk == 0 and n == 0, stop=kk == GROUP - 1 and n == 2),
                                    tiles2[kk][1], h_ready[(kk, t // TPB)], bank.free)
                        yield a
                        cols = slice(half * BANK, (half + 1) * BANK)
                        x = dve(tensor_tensor(hid[:, t, cols], hid[:, t, cols], bank.ap[:, :], ALU.add), a, acc_ready[t])
                        bank.release(x)
                    acc_ready[t] = x
                    if g + GROUP >= JT:
                        stores.append(sp.dma(sem(f"s_out{t}"), dma_start(out[t], hid[:, t, :]), x))
                for kk in range(GROUP):
                    tiles2[kk][0].release(a)
                    h_free[kk] = [a]

        weave([products(), chain(normalise(t) for t in tiles[0::2]), chain(normalise(t) for t in tiles[1::2])]
              + [prepare() for _ in raw_slots_f])
        sp_end = flat(stores)

        values = {}
        for q in (sp, pe, act, dve, pool):
            q.number(values)
        block = whole.enter_context(nc.Block())

        @block.sync
        def _(eng):
            sp.play(eng)
            for t in sp_end:
                eng.wait_ge(t.sem, t.value)

        @block.tensor
        def _(eng):
            pe.play(eng)

        @block.scalar
        def _(eng):
            act.play(eng)

        @block.vector
        def _(eng):
            dve.play(eng)

        @block.gpsimd
        def _(eng):
            pool.play(eng)


def _h_order(a, axis):
    a = np.moveaxis(a, axis, 0)
    a = a.reshape(HS, RH, *a.shape[1:]).swapaxes(0, 1).reshape(H, *a.shape[1:])
    return np.moveaxis(a, 0, axis)


def _f_order(a, axis):
    a = np.moveaxis(a, axis, 0)
    a = a.reshape(HS, RH, C, *a.shape[1:]).transpose(2, 1, 0, *range(3, a.ndim + 2)).reshape(HID, *a.shape[1:])
    return np.moveaxis(a, 0, axis)


def _tiles(a):
    return a.reshape(-1, P, *a.shape[1:]).swapaxes(0, 1)


def _device_arrays(x, pos, ctx, rat_in, rat_out, ffn):
    d = {"x": _f_order(x.reshape(TILES * P, HID), 1).reshape(TILES, P, HID), "pos": pos.reshape(TILES, P).T}
    in_w = np.concatenate([_h_order(rat_in["attn_w"], 0), _h_order(rat_in["mlp_w"], 0)], axis=1)
    d["inw"] = _tiles(in_w).transpose(0, 1, 3, 2).reshape(P, -1)
    gamma = np.concatenate([rat_in["attn_g"], rat_in["mlp_g"]]).reshape(5, H)
    beta = np.concatenate([rat_in["attn_b"], rat_in["mlp_b"]]).reshape(5, H)
    gb = np.stack([_h_order(gamma, 1), _h_order(beta, 1)], axis=-1)
    d["gb"] = gb.reshape(5, HH, P, 2).transpose(2, 1, 0, 3)
    d["wqkv"] = _tiles(_h_order(rat_in["qkv"], 2).reshape(3 * H, H).T)
    d["ctx"] = _tiles(_h_order(ctx, 2).transpose(2, 0, 1))
    for n, w in enumerate(rat_out):
        ab, bias = w["wab"], w["wab_b"]
        def by_c(a):
            return a.reshape(RH, C - 1, *a.shape[1:]).swapaxes(0, 1).reshape(a.shape)
        rows = [_h_order(w["wod"][:H], 0), by_c(ab[:NA]), by_c(ab[NA:2 * NA]), ab[2 * NA:], w["wod"][H:]]
        d[f"wcat{n}"] = _tiles(np.concatenate(rows).T)
        row = np.concatenate([by_c(bias[:NA]), by_c(bias[NA:2 * NA]), bias[2 * NA:], np.zeros(DR, bias.dtype)])
        d[f"bias_ab{n}"] = np.tile(row, (P, 1))
        d[f"dut{n}"] = _h_order(w["du"], 0).T
        d[f"dub{n}"] = np.tile(_h_order(w["du_b"], 0), (P, 1))
    for k, w in ffn.items():
        if k.endswith("w2"):
            d[k] = _f_order(w, 0).T.reshape(JT, P, HID)
        else:
            d[k] = _f_order(w, 1).reshape(JT, P, KF, P).transpose(0, 3, 2, 1).reshape(JT, P, HID)
    d["ident"] = np.eye(P, dtype=np.float32)
    q, k = np.arange(P)[:, None], np.arange(P)[None, :]
    d["cmask"] = np.where(k > q, np.float32(MASKED), np.float32(0)).astype(np.float32)
    half = np.arange(HALF, dtype=np.float32) / np.float32(HALF)
    d["inv_freq"] = np.tile((np.float32(1) / np.power(np.float32(10000), half)).astype(np.float32), (P, 1))
    return {k: np.ascontiguousarray(v) for k, v in d.items()}


def kernel(**inputs):
    import concourse.bacc as bacc
    from concourse.bass_utils import run_bass_kernel_spmd

    i = {k: np.asarray(v) for k, v in inputs.items()}
    a = {k[len("L0_xattn_"):]: v for k, v in i.items() if k.startswith("L0_xattn_")}
    d = _device_arrays(
        i["x"], i["pos_BxS"], i["ctx_1024"],
        {"attn_w": a["attn_read_w"], "attn_g": a["attn_read_g"], "attn_b": a["attn_read_b"], "qkv": a["qkv_w"],
         "mlp_w": a["mlp_read_w"], "mlp_g": a["mlp_read_g"], "mlp_b": a["mlp_read_b"]},
        [{"wod": a[f"{n}_wod_w"], "wab": a[f"{n}_wab_w"], "wab_b": a[f"{n}_wab_b"], "du": a[f"{n}_du_w"],
          "du_b": a[f"{n}_du_b"]} for n in ("attn", "mlp")],
        {k[len("L0_ffn_"):]: v for k, v in i.items() if k.startswith("L0_ffn_")})
    nc = bacc.Bacc("TRN2", target_bir_lowering=False, num_devices=1)
    arrays = {f"in_{k}": v for k, v in d.items()}
    aps = {k: nc.dram_tensor(f"in_{k}", v.shape, mybir.dt.from_np(v.dtype), kind="ExternalInput").ap() for k, v in d.items()}
    out = nc.dram_tensor("out", (TILES, P, HID), F32, kind="ExternalOutput").ap()
    bass_layer(nc, aps, out)
    r = run_bass_kernel_spmd(nc, [arrays], core_ids=[0])
    y = np.asarray(r.results[0]["out"]).reshape(BATCH, SEQ, C, RH, HS)
    return np.ascontiguousarray(y.transpose(0, 1, 4, 3, 2)).reshape(BATCH, SEQ, HID)
```

```python
from contextlib import ExitStack

import numpy as np

import concourse.bass as bass
from concourse import mybir

F32 = mybir.dt.float32
F32R = mybir.dt.float32r
BF16 = mybir.dt.bfloat16
I32 = mybir.dt.int32
ALU = mybir.AluOpType
ACT = mybir.ActivationFunctionType
AX = mybir.AxisListType

P = 128
BATCH, SEQ, HID = 2, 512, 1024
H, C, RH = 256, 4, 16
HS = H // RH
DR, M, NH = 8, 1024, 16
WAYS = (3, 2)
HD = H // NH
HALF = HD // 2
INTER = 3584
TILES = BATCH * SEQ // P
TPB = SEQ // P
HH = H // P
KF = HID // P
MT = M // P
JT = INTER // P
BANK = 512
NA = (C - 1) * RH
NAB = 2 * NA + RH
NZ = H + NAB + DR
EPS = 1e-5
SSM_EPS = 1e-5
MASKED = -1e30
GROUP = 2
PARTS = 4
TWO_PI_BITS = 9
SIDE_LEAD = 500.0
LN_EXP = "natural_log_exp_and_others"


def two_pi_parts():
    left, parts = 2 * np.pi, []
    for _ in range(3):
        step = 2.0 ** (np.floor(np.log2(left)) - (TWO_PI_BITS - 1))
        parts.append(float(np.floor(left / step) * step))
        left -= parts[-1]
    return parts + [float(np.float32(left))]


class Token:

    def __init__(self, sem, step, about):
        self.sem, self.step, self.used, self.value, self.about = sem, step, False, None, about


class Queue:

    def __init__(self, sem, slowness=1.0):
        self.sem, self.items, self.clock, self.slowness = sem, [], 0.0, slowness

    def add(self, op, after, sem, step):
        issue, cost = op
        after = flat(after)
        for t in after:
            t.used = True
        start = max([self.clock] + [t.about for t in after])
        if step == 1:
            self.clock = start + cost * self.slowness
            done = Token(sem, step, self.clock + 60)
        else:
            self.clock = start + cost - 2000
            done = Token(sem, step, start + cost)
            done.used = True
        self.items.append((issue, after, done))
        return done

    def __call__(self, op, *after):
        return self.add(op, after, self.sem, 1)

    def dma(self, sem, op, *after):
        return self.add(op, after, sem, 16)

    def number(self, values):
        for _, _, done in self.items:
            if done.used:
                values[done.sem] = values.get(done.sem, 0) + done.step
                done.value = values[done.sem]

    def play(self, eng):
        seen = {}
        for issue, after, done in self.items:
            need = {}
            for t in after:
                need[t.sem] = max(need.get(t.sem, 0), t.value)
            for sem, value in need.items():
                if seen.get(sem, 0) < value:
                    eng.wait_ge(sem, value)
                    seen[sem] = value
            ins = issue(eng)
            if done.used:
                ins.then_inc(done.sem, done.step)


def flat(tokens):
    out = []
    for t in tokens:
        if isinstance(t, Token):
            out.append(t)
        elif t is not None:
            out += flat(t)
    return out


class Slot:

    def __init__(self, ap, sem=None):
        self.ap, self.sem, self.free, self.held = ap, sem, [], False

    def release(self, *tokens):
        self.free, self.held = list(tokens), False


class Ring:

    def __init__(self, slots):
        self.slots = slots

    def take(self):
        while all(s.held for s in self.slots):
            yield
        return self.now()

    def now(self):
        s = next(s for s in self.slots if not s.held)
        s.held = True
        self.slots = [x for x in self.slots if x is not s] + [s]
        return s


def columns(ap):
    return int(np.prod(ap.shape[1:]))


def matmul(out, lhsT, rhs, **options):
    passes = 4 if rhs.dtype == F32 else 1
    return lambda eng: eng.matmul(out, lhsT, rhs, **options), passes * max(64, columns(out)) / 2.4


def transpose(out, in_, identity):
    return lambda eng: eng.transpose(out, in_, identity), 107


def activation(out, in_, func, **options):
    return lambda eng: eng.activation(out, in_, func, **options), 190 + columns(in_) / 1.2


def elementwise(emit, out, rate=1.0):
    return emit, 70 + columns(out) / 0.96 * rate


def tensor_tensor(out, in0, in1, op):
    return elementwise(lambda eng: eng.tensor_tensor(out, in0, in1, op), out)


def tensor_scalar(out, in0, scalar1, scalar2, *ops):
    return elementwise(lambda eng: eng.tensor_scalar(out, in0, scalar1, scalar2, *ops), out)


def scalar_tensor_tensor(out, in0, scalar, in1, op0, op1):
    return elementwise(lambda eng: eng.scalar_tensor_tensor(out, in0, scalar, in1, op0, op1), out)


def tensor_copy(out, in_):
    return elementwise(lambda eng: eng.tensor_copy(out, in_), out)


def tensor_reduce(out, in_, axis, op, **options):
    return elementwise(lambda eng: eng.tensor_reduce(out, in_, axis, op, **options), in_)


def reciprocal(out, in_):
    return elementwise(lambda eng: eng.reciprocal(out, in_), out)


def bn_stats(out, in_):
    return elementwise(lambda eng: eng.bn_stats(out, in_), in_)


def bn_aggr(out, in_):
    return elementwise(lambda eng: eng.bn_aggr(out, in_), in_)


def memset(out, value):
    return elementwise(lambda eng: eng.memset(out, value), out)


def load_table(name):
    return lambda eng: eng.preload_act_table_set(name), 1300


def dma_start(out, in_):
    return lambda eng: eng.dma_start(out, in_), columns(out) * P * 4 / 350 + 2000


def weave(lanes, lead={}):
    when = {n: 0.0 for n in range(len(lanes))}
    now, idle = 0.0, 0
    while when:
        n = min(when, key=lambda k: (when[k] - lead.get(k, 0.0), k))
        now = max(now, when[n])
        try:
            tokens = next(lanes[n])
        except StopIteration:
            del when[n]
            continue
        idle = idle + 1 if tokens is None else 0
        assert idle < 100000, "the lanes hold each other up"
        if tokens is None:
            when[n] = now + 50.0
        else:
            when[n] = max([t.about for t in flat([tokens])], default=now)


def drained(lane):
    while True:
        try:
            next(lane)
        except StopIteration as end:
            return end.value


def bass_layer(nc: bass.Bass, d: dict, out: bass.AP):
    with ExitStack() as whole:
        def sem(name):
            return whole.enter_context(nc.semaphore(name))

        def sb(stack, name, shape, dt=F32):
            return stack.enter_context(nc.sbuf_tensor(name, shape, dt))

        pe, act, dve = (Queue(sem(n)) for n in ("s_pe", "s_act", "s_dve"))
        pool = Queue(sem("s_pool"), slowness=2.1)
        sp = Queue(sem("s_sp"))

        hid = sb(whole, "hid", [P, TILES, HID])
        ident = sb(whole, "ident", [P, P])
        coeff = sb(whole, "coeff", [P, 3])
        eps = sb(whole, "eps", [P, 1])
        x2_stat = sb(whole, "x2_stat", [P, TILES, 16])

        pairs = Ring([Slot(whole.enter_context(nc.psum_tensor(f"pair{n}", [P, 2, BANK], F32)))
                      for n in range(2)])
        banks = [whole.enter_context(nc.psum_tensor(f"bank{n}", [P, BANK], F32)) for n in range(4)]
        singles = Ring([Slot(b) for b in banks[:3]])
        obank = Slot(banks[3])

        e_eps = pool(memset(eps[:, :], EPS))

        names = ("w1", "w3", "w2")

        def raw_slot(stack, name, width):
            return Slot([sb(stack, f"{name}_{k}", [P, width]) for k in ("w", "base")], sem(f"s_{name}"))

        def load_raw(which, j, cols, slot):
            w, base = slot.ap
            sp.dma(slot.sem, dma_start(w[:, :], d[which][j][:, cols]), slot.free)
            return sp.dma(slot.sem, dma_start(base[:, :], d["mean_" + which][j][:, cols]), slot.free)

        attention = whole.enter_context(ExitStack())

        def sba(name, shape, dt=F32):
            return sb(attention, name, shape, dt)

        def load(name, buf, src):
            return sp.dma(sem("s_ld_" + name), dma_start(buf, src))

        l_ident = load("ident", ident[:, :], d["ident"])
        big = [sba(f"big{b}", [P, 8, SEQ]) for b in range(BATCH)]
        cmask = big[1][:, 0, 0:P]
        l_cmask = load("cmask", cmask, d["cmask"])
        pos_i = sba("pos_i", [P, TILES], I32)
        l_pos = load("pos", pos_i[:, :], d["pos"])
        inv = sba("inv", [P, HALF])
        l_inv = load("inv", inv[:, :], d["inv_freq"])
        gb = sba("gb", [P, HH, 5, 2])
        l_gb = load("gb", gb[:, :, :, :], d["gb"])
        x_loaded = []
        for t in range(TILES):
            x_loaded.append(sp.dma(sem(f"s_x{t}"), dma_start(hid[:, t, :], d["x"][t])))
            if t == 0:
                w_in = [sba(f"w_in{n}", [P, C, ways, H]) for n, ways in enumerate(WAYS)]
                l_in = [load("w_in0", w_in[0][:, :, :, :], d["w_in0"])]
                wqkv = sba("wqkv", [P, HH, 3 * H])
                l_wqkv = load("wqkv", wqkv[:, :, :], d["wqkv"])
        wcat, l_wcat, bias_ab, l_bias, dut, l_dut = [], [], [], [], [], []
        for n, kt in enumerate((HH, MT)):
            wcat.append(sba(f"wcat{n}", [P, kt, NZ]))
            l_wcat.append(load(f"wcat{n}", wcat[n][:, :, :], d[f"wcat{n}"]))
            bias_ab.append(sba(f"bias_ab{n}", [P, NAB + DR]))
            l_bias.append(load(f"bias_ab{n}", bias_ab[n][:, :], d[f"bias_ab{n}"]))
            dut.append(sba(f"dut{n}", [DR + 1, H]))
            l_dut.append(load(f"dut{n}", dut[n][:, :], d[f"dut{n}"]))
        l_in.append(load("w_in1", w_in[1][:, :, :, :], d["w_in1"]))
        ctxw = sba("ctxw", [P, HH, 2, M])
        l_ctx = load("ctx", ctxw[:, :, :, :], d["ctx"])

        identb = sba("identb", [P, P], BF16)
        maskb = sba("maskb", [P, P], BF16)
        e_maskb = [dve(tensor_copy(identb[:, :], ident[:, :]), l_ident),
                   dve(tensor_copy(maskb[:, :], cmask), l_cmask)]

        rope = big[1][:, 1, 0:4 * TILES * HALF].rearrange("p (n t f) -> p n t f", n=4, t=TILES)
        rcos = sba("rcos", [P, TILES, 2, HALF])
        rsin = sba("rsin", [P, TILES, 2, HALF])
        posf = sba("posf", [P, TILES])
        ang, turns, half_sin, whole_sin = (rope[:, n, :, :] for n in range(4))
        magic = float(1.5 * 2 ** 23)
        t = dve(tensor_copy(posf[:, :], pos_i[:, :]), l_pos)
        t = dve(tensor_tensor(ang, posf[:, :].unsqueeze(2).to_broadcast([P, TILES, HALF]),
                                          inv[:, :].unsqueeze(1).to_broadcast([P, TILES, HALF]), ALU.mult), t, l_inv)
        t = dve(tensor_scalar(turns, ang, float(1 / (2 * np.pi)), magic, ALU.mult, ALU.add), t)
        t = dve(tensor_scalar(turns, turns, -magic, None, ALU.add), t)
        for part in two_pi_parts():
            t = dve(scalar_tensor_tensor(ang, turns, -part, ang, ALU.mult, ALU.add), t)
        t = dve(tensor_scalar(ang, ang, 3.1415925, -3.1415925, ALU.min, ALU.max), t)
        t1 = act(activation(whole_sin, ang, ACT.Sin), t)
        t2 = act(activation(half_sin, ang, ACT.Sin, scale=0.5), t)
        t3 = dve(tensor_tensor(half_sin, half_sin, half_sin, ALU.mult), t2)
        e_rope = []
        for n in range(2):
            e_rope.append(dve(tensor_scalar(rcos[:, :, n, :], half_sin, -2.0, 1.0, ALU.mult, ALU.add), t3))
            e_rope.append(dve(tensor_scalar(rsin[:, :, n, :], whole_sin, 2.0 * n - 1.0, None, ALU.mult), t1))

        qkv_bias = sba("qkv_bias", [P, 3 * H])
        ones = sba("ones", [P, P])
        e_ones = pool(memset(ones[:, :], 1.0))
        e_qkv = []

        def fold_qkv():
            yield l_gb
            pq = yield from pairs.take()
            for hh in range(HH):
                for o in range(3):
                    last = dve(tensor_scalar(big[0][:, hh, o * P:(o + 1) * P], ones[:, :], gb[:, hh, o, 1:2], None, ALU.mult),
                               e_ones, l_gb)
            yield last, l_wqkv
            for o in range(3):
                for hh in range(HH):
                    t = pe(matmul(pq.ap[:, o // 2, (o % 2) * H:(o % 2 + 1) * H], big[0][:, hh, o * P:(o + 1) * P],
                                  wqkv[:, hh, o * H:(o + 1) * H], start=hh == 0, stop=hh == HH - 1),
                           last, l_wqkv, pq.free)
            yield t
            folded = [act(activation(qkv_bias[:, 0:2 * H], pq.ap[:, 0, :], ACT.Copy), t),
                      act(activation(qkv_bias[:, 2 * H:], pq.ap[:, 1, 0:H], ACT.Copy), t)]
            pq.release(folded)
            for hh in range(HH):
                for o in range(3):
                    folded.append(pool(tensor_scalar(
                        wqkv[:, hh, o * H:(o + 1) * H], wqkv[:, hh, o * H:(o + 1) * H], gb[:, hh, o, 0:1], None, ALU.mult), t))
            e_qkv.extend(folded)

        mlp_bias = sba("mlp_bias", [P, 2, MT])
        e_ctx = []

        def fold_ctx():
            yield l_ctx
            pq = yield from pairs.take()
            for g in range(2):
                for m in range(MT):
                    for hh in range(HH):
                        t = pe(matmul(
                            pq.ap[:, 0, g * MT + m:g * MT + m + 1], ctxw[:, hh, g, m * P:(m + 1) * P],
                            gb[:, hh, 3 + g, 1:2], start=hh == 0, stop=hh == HH - 1), l_ctx, l_gb, pq.free)
            yield t
            a = act(activation(mlp_bias[:, :, :], pq.ap[:, 0, 0:2 * MT].rearrange("p (g m) -> p g m", g=2), ACT.Copy), t)
            pq.release(a)
            folded = [a]
            for hh in range(HH):
                for g in range(2):
                    folded.append(pool(tensor_scalar(
                        ctxw[:, hh, g, :], ctxw[:, hh, g, :], gb[:, hh, 3 + g, 0:1], None, ALU.mult), t))
                    yield folded[-1]
            e_ctx.extend(folded)

        terms = Ring([Slot(sba(f"terms{n}", [P, 2 * 3 * H]), sem(f"s_terms{n}")) for n in range(1)])
        yT = Ring([Slot(sba(f"yT{n}", [P, 3 * HH, P])) for n in range(3)])
        qk = Ring([Slot((sba("qk", [P, 2 * H]), sba("wideqk", [P, 2 * NH, 2 * HD])))])
        v = sba("v", [P, TILES, H])
        prob = Ring([Slot(sba(f"prob{n}", [P, BANK])) for n in range(2)])
        probT = Ring([Slot(sba(f"probT{n}", [P, BANK])) for n in range(2)])
        stats = Ring([Slot(sba(f"stat{n}", [P, 24])) for n in range(4)])
        negmax = sba("negmax", [P, 2, NH])
        sums = sba("sums", [P, 2, NH])
        o_sb = Ring([Slot(sba("o_sb", [P, H]))])
        inT = [sba("inT", [P, 2 * HH, SEQ])]
        wr = Ring([Slot({k: sba(f"wr_{k}{n}", [P, w]) for k, w in
                         (("z", H + NA), ("b", NAB + DR), ("out", H), ("r", NA),
                          ("a", 3 * H), ("dl", P))}) for n in range(2)])
        e_dl = [pool(memset(s.ap["dl"][:, :], 1.0)) for s in wr.slots]

        def rsqrt_of(var, n, scratch, after):
            lnv, y = scratch[:, 0:n], scratch[:, n:2 * n]
            t = act(activation(lnv, var, ACT.Ln, bias=eps[:, 0:1]), after, e_eps)
            t = act(activation(y, lnv, ACT.Exp, scale=-0.5), t)
            yield t
            t = dve(tensor_tensor(lnv, y, y, ALU.mult), t)
            t = dve(scalar_tensor_tensor(lnv, var, EPS, lnv, ALU.add, ALU.mult), t)
            t = dve(tensor_scalar(lnv, lnv, -0.5, 1.5, ALU.mult, ALU.add), t)
            return dve(tensor_tensor(y, y, lnv, ALU.mult), t), y

        def layernorm(t, target, after):
            slot = yield from stats.take()
            st = slot.ap
            a = [dve(bn_stats(st[:, 6 * n:6 * n + 6], hid[:, t, n * BANK:(n + 1) * BANK]), after, slot.free) for n in range(2)]
            a = dve(bn_aggr(st[:, 12:14], st[:, 0:12]), a)
            yield a
            a, r = yield from rsqrt_of(st[:, 13:14], 1, st[:, 14:16], a)
            a = dve(tensor_scalar(target, hid[:, t, :], st[:, 12:13], r, ALU.subtract, ALU.mult), a)
            slot.release(a)
            return a

        def turn_blocks(source, blocks, pair, after):
            for k in range(blocks):
                a = pe(transpose(pair.ap[:, k // 4, (k % 4) * P:(k % 4 + 1) * P], source[:, k, :], ident[:, :]), after, pair.free, l_ident)
            return a

        def rat_in(t, n, ways, after):
            term = yield from terms.take()
            y = yield from yT.take()
            total = y.ap[:, 0:ways * HH, :].rearrange("p (o a) m -> p o (a m)", o=ways)
            t1, t2 = (term.ap[:, m * ways * H:(m + 1) * ways * H].rearrange("p (o h) -> p o h", o=ways) for m in range(2))
            yield after

            def product(c, target):
                x = hid[:, t, c * H:(c + 1) * H].unsqueeze(1).to_broadcast([P, ways, H])
                return tensor_tensor(target, x, w_in[n][:, c, :, :], ALU.mult)

            p3 = pool(product(3, t2), after, l_in[n], term.free)
            a = dve(product(0, total), after, l_in[n], y.free)
            for c in (1, 2):
                m = dve(product(c, t1), after, l_in[n], term.free, a)
                a = dve(tensor_tensor(total, total, t1, ALU.add), m, a)
                yield a
            a = dve(tensor_tensor(total, total, t2, ALU.add), a, p3)
            term.release(a)
            yield a
            slot = yield from stats.take()
            st = slot.ap
            s = [dve(bn_stats(st[:, 6 * o:6 * o + 6], total[:, o, :]), a, slot.free) for o in range(ways)]
            s = [dve(bn_aggr(st[:, 18 + 2 * o:20 + 2 * o], st[:, 6 * o:6 * o + 6]), s) for o in range(ways)]
            yield s
            mv = st[:, 18:24].rearrange("p (o two) -> p o two", two=2)
            s, r = yield from rsqrt_of(mv[:, 0:ways, 1:2].rearrange("p o x -> p (o x)"), ways, st[:, 0:6], s)
            s = [dve(tensor_scalar(total[:, o, :], total[:, o, :], st[:, 18 + 2 * o:19 + 2 * o], r[:, o:o + 1],
                                   ALU.subtract, ALU.mult), s) for o in range(ways)]
            slot.release(s)
            yield s
            pair = yield from pairs.take()
            a = turn_blocks(y.ap, ways * HH, pair, s)
            yield a
            return y, pair, a

        q_ready = [None] * TILES

        def front(t):
            b, col = t // TPB, (t % TPB) * P
            yield x_loaded[t]
            ln = yield from layernorm(t, hid[:, t, :], x_loaded[t])
            yield ln
            y, pair, a = yield from rat_in(t, 0, 3, ln)
            ev = [act(activation(y.ap[:, 0:4, :], pair.ap[:, 0, :].rearrange("p (a b) -> p a b", a=4), ACT.Copy), a),
                  act(activation(y.ap[:, 4:6, :], pair.ap[:, 1, 0:2 * P].rearrange("p (a b) -> p a b", a=2), ACT.Copy), a)]
            pair.release(ev)
            yield ev
            while not e_qkv:
                yield None
            s = yield from qk.take()
            pair = yield from pairs.take()
            for o in range(3):
                for hh in range(HH):
                    a = pe(matmul(pair.ap[:, o // 2, (o % 2) * H:(o % 2 + 1) * H], y.ap[:, o * HH + hh, :],
                                  wqkv[:, hh, o * H:(o + 1) * H], start=hh == 0, stop=hh == HH - 1),
                           ev, e_qkv, pair.free)
            y.release(a)
            yield a
            plain, wide = s.ap
            e1 = dve(tensor_tensor(plain[:, :], pair.ap[:, 0, :], qkv_bias[:, 0:2 * H], ALU.add), a, s.free, e_qkv)
            e2 = dve(tensor_tensor(v[:, t, :], pair.ap[:, 1, 0:H], qkv_bias[:, 2 * H:], ALU.add), a, e_qkv)
            pair.release(e1, e2)
            yield e1
            halves = plain[:, :].rearrange("p (g two f) -> p g two f", two=2, f=HALF)
            by_head = plain[:, :].rearrange("p (g f) -> p g f", f=HD)
            e3 = [dve(tensor_tensor(wide[:, :, HD + n * HALF:HD + (n + 1) * HALF], halves[:, :, 1 - n, :],
                                    rsin[:, t, n, :].unsqueeze(1).to_broadcast([P, 2 * NH, HALF]), ALU.mult), e1, s.free, e_rope)
                  for n in range(2)]
            e4 = dve(tensor_tensor(by_head, by_head, rcos[:, t, :, :].rearrange("p a b -> p (a b)").unsqueeze(1).to_broadcast([P, 2 * NH, HD]),
                                   ALU.mult), e3)
            yield e4
            e5 = dve(tensor_tensor(wide[:, :, 0:HD], by_head, wide[:, :, HD:], ALU.add), e4)
            yield e5
            pair = yield from pairs.take()
            a = turn_blocks(wide[:, :, :].rearrange("p (k a) b -> p k (a b)", a=4), 8, pair, e5)
            s.release(a)
            yield a
            ev = [act(activation(big[b][:, 4 * n:4 * n + 4, col:col + P], pair.ap[:, n, :].rearrange("p (a b) -> p a b", a=4), ACT.Copy,
                                 scale=(HD ** -0.5, 1.0)[n]), a, e_qkv) for n in range(2)]
            pair.release(ev)
            q_ready[t] = ev + [e2]

        att_ready = [None] * TILES

        def attend(t):
            b, i = t // TPB, t % TPB
            while any(q_ready[b * TPB + k] is None for k in range(i + 1)):
                yield None
            ready = [q_ready[b * TPB + k] for k in range(i + 1)]
            yield ready
            n = (i + 1) * P
            per = max(1, BANK // n)
            par = t % 2
            order = [4 * q + r for r in range(4) for q in range(4)] if per > 1 else list(range(NH))
            groups = [order[g:g + per] for g in range(0, NH, per)]
            held = {}

            def scores(g):
                s = yield from singles.take()
                for u, h in enumerate(groups[g]):
                    row = (h % 4) * 32
                    pe(matmul(s.ap[:, u * n:(u + 1) * n], big[b][row:row + HD, h // 4, i * P:(i + 1) * P],
                              big[b][row:row + HD, 4 + h // 4, 0:n], start=True, stop=False), ready, s.free)
                    a = pe(matmul(s.ap[:, (u + 1) * n - P:(u + 1) * n], identb[:, :], maskb[:, :], start=False, stop=True), e_maskb)
                held[g] = (s, a)

            def soften(g):
                s, a = held[g]
                h0 = g * per
                m = dve(tensor_reduce(negmax[:, par, h0:h0 + per], s.ap[:, 0:per * n].rearrange("p (u n) -> p u n", u=per),
                                      AX.X, ALU.max, negate=True), a)
                p = yield from prob.take()
                for u, h in enumerate(groups[g]):
                    a = act(activation(p.ap[:, u * n:(u + 1) * n], s.ap[:, u * n:(u + 1) * n], ACT.Exp,
                                       bias=negmax[:, par, h0 + u:h0 + u + 1], accum_out=sums[:, par, h0 + u:h0 + u + 1]), m, p.free)
                s.release(a)
                held[g] = (p, a)

            def turn(g):
                p, a = held[g]
                s = yield from singles.take()
                for k in range(per * (i + 1)):
                    x = pe(transpose(s.ap[:, k * P:(k + 1) * P], p.ap[:, k * P:(k + 1) * P], ident[:, :]), a, s.free)
                p.release(x)
                q = yield from probT.take()
                w = per * n
                if g % 2:
                    x = dve(tensor_copy(q.ap[:, 0:w], s.ap[:, 0:w]), x, q.free)
                else:
                    x = act(activation(q.ap[:, 0:w], s.ap[:, 0:w], ACT.Copy), x, q.free)
                s.release(x)
                held[g] = (q, x)

            def gather(g):
                q, a = held.pop(g)
                for u, h in enumerate(groups[g]):
                    for k in range(i + 1):
                        x = pe(matmul(obank.ap[:, h * HD:(h + 1) * HD], q.ap[:, (u * (i + 1) + k) * P:(u * (i + 1) + k + 1) * P],
                                      v[:, b * TPB + k, h * HD:(h + 1) * HD], start=k == 0, stop=k == i), a, ready, obank.free)
                q.release(x)
                return x

            last = len(groups)
            for g in range(last + 2):
                if g < last:
                    yield from scores(g)
                    yield held[g][1]
                if 0 <= g - 2 < last:
                    x = gather(g - 2)
                if g < last:
                    yield from soften(g)
                if 0 <= g - 1 < last:
                    yield held[g - 1][1]
                    yield from turn(g - 1)
            yield x
            o = yield from o_sb.take()
            r = dve(reciprocal(sums[:, par, :], sums[:, par, :]), x)
            by_head = sums[:, par, :].rearrange("p (r q) -> p q r" if per > 1 else "p (q r) -> p q r", q=4)
            r = dve(tensor_tensor(o.ap[:, :].rearrange("p (q r f) -> p q r f", q=4, f=HD),
                                  obank.ap[:, 0:H].rearrange("p (q r f) -> p q r f", q=4, f=HD),
                                  by_head.unsqueeze(3).to_broadcast([P, 4, 4, HD]), ALU.mult), r, o.free)
            obank.release(r)
            yield r
            y = yield from yT.take()
            s = yield from singles.take()
            for hh in range(HH):
                a = pe(transpose(s.ap[:, hh * P:(hh + 1) * P], o.ap[:, hh * P:(hh + 1) * P], ident[:, :]), r, s.free)
            o.release(a)
            yield a
            a = act(activation(y.ap[:, 0:HH, :], s.ap[:, 0:HH * P].rearrange("p (a b) -> p a b", a=HH), ACT.Copy), a, y.free)
            s.release(a)
            att_ready[t] = (y, a)

        def rat_out(t, n, kt, blocks, after, done_with, h_ready):
            pair = yield from pairs.take()
            for k in range(kt):
                a = pe(matmul(pair.ap[:, 0, 0:NZ], blocks[:, k, :], wcat[n][:, k, :], start=k == 0, stop=k == kt - 1),
                       after, l_wcat[n], pair.free)
            if done_with is not None:
                done_with.release(a)
            yield a
            w = yield from wr.take()
            z, bb, ov, rr, aa, dl = (w.ap[k] for k in ("z", "b", "out", "r", "a", "dl"))
            ez = aa[:, 0:H + NA]
            f = w.free
            e1 = dve(tensor_tensor(bb[:, :], pair.ap[:, 0, H:NZ], bias_ab[n][:, :], ALU.add), a, f, l_bias[n])
            e2 = act(activation(ov[:, :], pair.ap[:, 0, 0:H], ACT.Copy), a, f, e1)
            yield e1
            a = pe(transpose(pair.ap[0:DR, 1, 0:P], bb[:, NAB:NAB + DR], ident[:, :]), e1)
            yield a
            a = act(activation(dl[0:DR, :], pair.ap[0:DR, 1, 0:P], ACT.Copy), a, f)
            yield a
            low = pair.ap[:, 1, P:P + H]
            a = pe(matmul(low, dl[0:DR + 1, :], dut[n][:, :], start=True, stop=True), a, e_dl, l_dut[n])
            yield a
            a = [act(activation(ez[:, 0:H], low, ACT.Abs), a, f), act(activation(ez[:, H:], bb[:, 0:NA], ACT.Abs), e1, f)]
            a = act(activation(ez[:, :], ez[:, :], ACT.Exp, scale=-1.0), a)
            a = act(activation(ez[:, :], ez[:, :], ACT.Ln, bias=1.0), a)
            yield a
            e5 = [dve(scalar_tensor_tensor(z[:, 0:H], low, 0.0, ez[:, 0:H], ALU.max, ALU.add), a, f),
                  dve(scalar_tensor_tensor(z[:, H:], bb[:, 0:NA], 0.0, ez[:, H:], ALU.max, ALU.add), a, f)]
            pair.release(e2, e5)
            delta, nega = z[:, 0:H], z[:, H:]
            wide = [P, C - 1, RH, HS]
            e6 = dve(tensor_tensor(aa[:, :].rearrange("p (c g s) -> p c g s", c=C - 1, s=HS),
                                   delta.rearrange("p (g s) -> p g s", s=HS).unsqueeze(1).to_broadcast(wide),
                                   nega.rearrange("p (c g) -> p c g", c=C - 1).unsqueeze(3).to_broadcast(wide), ALU.mult), e5, f)
            e7 = dve(tensor_scalar(rr[:, :], nega, -1.0, -SSM_EPS, ALU.mult, ALU.add), e5, f)
            e7 = dve(reciprocal(rr[:, :], rr[:, :]), e7)
            e7 = dve(tensor_tensor(rr[:, :], rr[:, :], bb[:, NA:2 * NA], ALU.mult), e7)
            yield e6
            e8 = act(activation(aa[:, :], aa[:, :], ACT.Exp, scale=-1.0), e6)
            skip = bb[:, 2 * NA:NAB]
            g = pool(tensor_tensor(delta.rearrange("p (g s) -> p g s", s=HS), delta.rearrange("p (g s) -> p g s", s=HS),
                                   skip.unsqueeze(2).to_broadcast([P, RH, HS]), ALU.mult), e6)
            g = pool(tensor_tensor(delta, delta, ov[:, :], ALU.mult), g, e2)
            g = pool(tensor_tensor(hid[:, t, 3 * H:], hid[:, t, 3 * H:], delta, ALU.add), g, h_ready)
            yield e8
            ha = hid[:, t, 0:3 * H]
            e9 = pool(tensor_tensor(ha, ha, aa[:, :], ALU.mult), e8, h_ready)
            yield e9
            groups = aa[:, :].rearrange("p (g s) -> p g s", s=HS)
            e10 = dve(scalar_tensor_tensor(groups, groups, -1.0, rr[:, :].unsqueeze(2).to_broadcast([P, NA, HS]),
                                           ALU.add, ALU.mult), e9, e7)
            by_c = aa[:, :].rearrange("p (c h) -> p c h", c=C - 1)
            e11 = dve(tensor_tensor(by_c, by_c, ov[:, :].unsqueeze(1).to_broadcast([P, C - 1, H]), ALU.mult), e10, e2)
            e12 = dve(tensor_tensor(ha, ha, aa[:, :], ALU.add), e11)
            w.release(e12, g, e7)
            return [e12, g]

        h2_ready = [None] * TILES
        inT_ready = [None] * TILES
        inT_free = []

        def back(t):
            while att_ready[t] is None:
                yield None
            y, a = att_ready[t]
            yield a
            h2 = yield from rat_out(t, 0, HH, y.ap, a, y, q_ready[t])
            h2_ready[t] = h2
            yield h2
            y, pair, a = yield from rat_in(t, 1, 2, h2)
            y.release(a)
            col = (t % TPB) * P
            while t >= TPB and not inT_free:
                yield None
            ev = act(activation(inT[0][:, :, col:col + P], pair.ap[:, 0, :].rearrange("p (a b) -> p a b", a=4), ACT.Copy),
                     a, inT_free if t >= TPB else [])
            pair.release(ev)
            inT_ready[t] = ev

        mlp_ready = [[], []]

        def mlp(b):
            while not e_ctx or any(inT_ready[t] is None for t in range(b * TPB, (b + 1) * TPB)):
                yield None
            ready = inT_ready[b * TPB:(b + 1) * TPB]
            yield ready
            for m in range(MT):
                pair = yield from pairs.take()
                s = yield from prob.take()
                for g in range(2):
                    for hh in range(HH):
                        a = pe(matmul(pair.ap[:, g, :], ctxw[:, hh, g, m * P:(m + 1) * P], inT[0][:, g * HH + hh, :],
                                      start=hh == 0, stop=hh == HH - 1), ready, e_ctx, pair.free)
                x = act(activation(s.ap[:, :], pair.ap[:, 0, :], ACT.Silu, bias=mlp_bias[:, 0, m:m + 1]), a, s.free, e_ctx)
                x = dve(scalar_tensor_tensor(big[b][:, m, :], pair.ap[:, 1, :], mlp_bias[:, 1, m:m + 1], s.ap[:, :],
                                             ALU.add, ALU.mult), x, [att_ready[t][1] for t in range(b * TPB, (b + 1) * TPB)])
                s.release(x)
                pair.release(x)
            act(load_table(LN_EXP))
            inT_free.append(a)
            mlp_ready[b] = [x]

        x2_ready = [None] * TILES

        def finish(t):
            b, col = t // TPB, (t % TPB) * P
            while not mlp_ready[b]:
                yield None
            yield mlp_ready[b]
            h3 = yield from rat_out(t, 1, MT, big[b][:, :, col:col + P], mlp_ready[b], None, h2_ready[t])
            yield h3
            xr = yield from terms.take()
            again = xr.ap[:, 0:HID]
            l = sp.dma(xr.sem, dma_start(again, d["x"][t]), xr.free)
            yield l
            a = pool(tensor_tensor(hid[:, t, :], hid[:, t, :], again, ALU.add), h3, l)
            xr.release(a)
            yield a
            st = x2_stat[:, t, :]
            s = [dve(bn_stats(st[:, 6 * n:6 * n + 6], hid[:, t, n * BANK:(n + 1) * BANK]), a) for n in range(2)]
            s = dve(bn_aggr(st[:, 12:14], st[:, 0:12]), s)
            yield s
            s, r = yield from rsqrt_of(st[:, 13:14], 1, st[:, 14:16], s)
            s = dve(tensor_scalar(st[:, 14:15], st[:, 12:13], r, -1.0, ALU.mult, ALU.mult), s)
            x2_ready[t] = [a, s]

        halves = HID // BANK
        absum = sba("absum", [P, 3, JT * halves])
        parts = Ring([raw_slot(attention, f"part{n}", BANK) for n in range(PARTS)])
        raw_done = []

        def measure():
            loads = []
            every = [(n, j, q) for n in range(3) for j in range(JT) for q in range(halves)]
            for k in range(len(every) + PARTS):
                if k >= PARTS:
                    n, j, q = every[k - PARTS]
                    s, l = loads[k - PARTS]
                    w, base = s.ap
                    yield l
                    a = pool(tensor_tensor(w[:, :], w[:, :], base[:, :], ALU.subtract), l)
                    yield a
                    a = act(activation(w[:, :], w[:, :], ACT.Abs,
                                       accum_out=absum[:, n, j * halves + q:j * halves + q + 1]), a)
                    s.release(a)
                    raw_done.append(a)
                if k < len(every):
                    n, j, q = every[k]
                    s = yield from parts.take()
                    loads.append((s, load_raw(names[n], j, slice(q * BANK, (q + 1) * BANK), s)))

        def chain(gens):
            for g in gens:
                yield from g

        act(load_table(LN_EXP))
        tiles = range(TILES)
        weave([chain(front(t) for t in tiles[0::2]), chain(front(t) for t in tiles[1::2]),
               chain(attend(t) for t in tiles),
               chain(back(t) for t in tiles[0::2]), chain(back(t) for t in tiles[1::2]),
               chain(mlp(b) for b in range(BATCH)),
               chain(finish(t) for t in tiles[0::2]), chain(finish(t) for t in tiles[1::2]),
               fold_ctx(), measure(), fold_qkv()], lead={8: SIDE_LEAD, 9: SIDE_LEAD})

        csum = sba("csum", [P, 3])
        s = singles.now()
        a = dve(tensor_reduce(csum[:, :], absum[:, :, :], AX.X, ALU.add), raw_done[-1])
        a = pe(matmul(s.ap[:, 0:3], ones[:, :], csum[:, :], start=True, stop=True), a, s.free, e_ones)
        e_coeff = dve(tensor_scalar(coeff[:, :], s.ap[:, 0:3], float(1.0 / (INTER * HID)), None, ALU.mult), a)
        s.release(e_coeff)
        over = [e_coeff, x2_ready[TILES - 1], act(activation(eps[:, :], eps[:, :], ACT.Copy), e_coeff, x2_ready)]
        attention.close()

        ffn = whole.enter_context(ExitStack())

        def sbf(name, shape, dt=F32):
            return sb(ffn, name, shape, dt)

        xnT = [sbf(f"xnT_{p}", [P, KF, TILES * P], F32R) for p in ("hi", "lo")]
        w13 = Ring([Slot([sbf(f"w13_{p}{n}", [P, KF, P], F32R) for p in ("hi", "lo")]) for n in range(3)])
        w2 = Ring([Slot([sbf(f"w2_{p}{n}", [P, HID], F32R) for p in ("hi", "lo")]) for n in range(GROUP + 1)])
        ht = [[sbf(f"h_{p}{k}", [P, TILES * P], F32R) for p in ("hi", "lo")] for k in range(GROUP)]
        works = Ring([Slot(sbf(f"work{n}", [P, HID])) for n in range(3)])
        sgf = Ring([Slot(sbf(f"sgf{n}", [P, BANK])) for n in range(2)])
        hf = Ring([Slot(sbf(f"hf{n}", [P, BANK])) for n in range(2)])
        raws = Ring([raw_slot(ffn, f"raw{n}", HID) for n in range(3)])
        for s in raws.slots:
            s.release(over)

        xn_ready = [None] * TILES

        def normalise(t):
            yield x2_ready[t]
            wk = yield from works.take()
            mean, shift, r = (x2_stat[:, t, c:c + 1] for c in (12, 14, 15))
            if t % 2:
                a = pool(tensor_scalar(wk.ap[:, :], hid[:, t, :], mean, r, ALU.subtract, ALU.mult), x2_ready[t], wk.free, over)
            else:
                a = act(activation(wk.ap[:, :], hid[:, t, :], ACT.Identity, bias=shift, scale=r), x2_ready[t], wk.free, over)
            yield a
            pair = yield from pairs.take()
            a = turn_blocks(wk.ap[:, :].rearrange("p (k f) -> p k f", f=P), KF, pair, a)
            wk.release(a)
            yield a
            turned = pair.ap[:, :, :].rearrange("p a (b c) -> p (a b) c", b=4)
            hi = act(activation(xnT[0][:, :, t * P:(t + 1) * P], turned, ACT.Copy), a, over)
            yield hi
            lo = dve(tensor_tensor(xnT[1][:, :, t * P:(t + 1) * P], turned,
                                   xnT[0][:, :, t * P:(t + 1) * P].bitcast(F32), ALU.subtract), hi)
            pair.release(lo)
            xn_ready[t] = lo

        need = [(which, j) for j in range(JT) for which in names]
        todo = iter(need)
        prepared = {}

        def prepare():
            for which, j in todo:
                s = yield from raws.take()
                l = load_raw(which, j, slice(0, HID), s)
                yield l
                w, bs = s.ap
                n = names.index(which)
                a = pool(tensor_tensor(w[:, :], w[:, :], bs[:, :], ALU.subtract), l)
                yield a
                a = act(activation(w[:, :], w[:, :], ACT.Sign), a)
                yield a
                a = dve(scalar_tensor_tensor(w[:, :], w[:, :], coeff[:, n:n + 1], bs[:, :], ALU.mult, ALU.add), a, e_coeff)
                yield a
                target = yield from (w2 if which == "w2" else w13).take()
                hi_, lo_ = (x[:, :, :].rearrange("p a b -> p (a b)") if which != "w2" else x[:, :] for x in target.ap)
                a = act(activation(hi_, w[:, :], ACT.Copy), a, target.free, over)
                yield a
                a = dve(tensor_tensor(lo_, w[:, :], hi_.bitcast(F32), ALU.subtract), a, target.free)
                s.release(a)
                prepared[(which, j)] = (target, a)

        def prepared_tile(key):
            while key not in prepared:
                yield None
            return prepared.pop(key)

        def passes(stat_parts, mov_parts):
            return [(stat_parts[0], mov_parts[0]), (stat_parts[1], mov_parts[0]), (stat_parts[0], mov_parts[1])]

        acc_ready = [x2_ready[t] for t in range(TILES)]
        h_free = [[] for _ in range(GROUP)]
        stores = []

        def products():
            for g in range(0, JT, GROUP):
                h_ready, gated = {}, {}
                for kk in range(GROUP):
                    j = g + kk
                    for which in ("w1", "w3"):
                        ws, e_w = yield from prepared_tile((which, j))
                        pair = yield from pairs.take()
                        for b in range(BATCH):
                            while None in xn_ready[:(b + 1) * TPB]:
                                yield None
                            for k in range(KF):
                                for n, (ww, xx) in enumerate(passes(ws.ap, xnT)):
                                    a = pe(matmul(
                                        pair.ap[:, b, :], ww[:, k, :], xx[:, k, b * SEQ:(b + 1) * SEQ],
                                        start=k == 0 and n == 0, stop=k == KF - 1 and n == 2),
                                        e_w, xn_ready[:(b + 1) * TPB], pair.free)
                            if b == BATCH - 1:
                                ws.release(a)
                            yield a
                            if which == "w1":
                                sg = sgf.now()
                                x = act(activation(sg.ap[:, :], pair.ap[:, b, :], ACT.Silu), a, sg.free)
                                gated[b] = (sg, x)
                            else:
                                sg, x = gated[b]
                                hs = hf.now()
                                x = dve(tensor_tensor(hs.ap[:, :], sg.ap[:, :], pair.ap[:, b, :], ALU.mult), a, x, hs.free)
                                sg.release(x)
                                yield x
                                cols = slice(b * SEQ, (b + 1) * SEQ)
                                y = act(activation(ht[kk][0][:, cols], hs.ap[:, :], ACT.Copy), x, h_free[kk], over)
                                yield y
                                z = dve(tensor_tensor(ht[kk][1][:, cols], hs.ap[:, :], ht[kk][0][:, cols].bitcast(F32),
                                                      ALU.subtract), y, h_free[kk])
                                hs.release(z)
                                h_ready[(kk, b)] = z
                        pair.release(x, gated[0][1])
                tiles2 = []
                for kk in range(GROUP):
                    tiles2.append((yield from prepared_tile(("w2", g + kk))))
                for t in range(TILES):
                    for half in range(2):
                        bank = yield from singles.take()
                        for kk in range(GROUP):
                            for n, (hh_, ww) in enumerate(passes(ht[kk], tiles2[kk][0].ap)):
                                a = pe(matmul(
                                    bank.ap[:, :], hh_[:, t * P:(t + 1) * P], ww[:, half * BANK:(half + 1) * BANK],
                                    start=kk == 0 and n == 0, stop=kk == GROUP - 1 and n == 2),
                                    tiles2[kk][1], h_ready[(kk, t // TPB)], bank.free)
                        yield a
                        cols = slice(half * BANK, (half + 1) * BANK)
                        x = dve(tensor_tensor(hid[:, t, cols], hid[:, t, cols], bank.ap[:, :], ALU.add), a, acc_ready[t])
                        bank.release(x)
                    acc_ready[t] = x
                    if g + GROUP >= JT:
                        stores.append(sp.dma(sem(f"s_out{t}"), dma_start(out[t], hid[:, t, :]), x))
                for kk in range(GROUP):
                    tiles2[kk][0].release(a)
                    h_free[kk] = [a]

        weave([products()] + [chain(normalise(t) for t in tiles[n::3]) for n in range(3)] +
              [prepare() for _ in raws.slots])
        sp_end = flat(stores)

        values = {}
        for q in (sp, pe, act, dve, pool):
            q.number(values)
        block = whole.enter_context(nc.Block())

        @block.sync
        def _(eng):
            sp.play(eng)
            for t in sp_end:
                eng.wait_ge(t.sem, t.value)

        @block.tensor
        def _(eng):
            pe.play(eng)

        @block.scalar
        def _(eng):
            act.play(eng)

        @block.vector
        def _(eng):
            dve.play(eng)

        @block.gpsimd
        def _(eng):
            pool.play(eng)


def _h_order(a, axis):
    a = np.moveaxis(a, axis, 0)
    a = a.reshape(HS, RH, *a.shape[1:]).swapaxes(0, 1).reshape(H, *a.shape[1:])
    return np.moveaxis(a, 0, axis)


def _f_order(a, axis):
    a = np.moveaxis(a, axis, 0)
    a = a.reshape(HS, RH, C, *a.shape[1:]).transpose(2, 1, 0, *range(3, a.ndim + 2)).reshape(HID, *a.shape[1:])
    return np.moveaxis(a, 0, axis)


def _tiles(a):
    return a.reshape(-1, P, *a.shape[1:]).swapaxes(0, 1)


def _device_arrays(x, pos, ctx, rat_in, rat_out, ffn):
    d = {"x": _f_order(x.reshape(TILES * P, HID), 1).reshape(TILES, P, HID), "pos": pos.reshape(TILES, P).T}
    in_w = np.concatenate([_h_order(rat_in["attn_w"], 0), _h_order(rat_in["mlp_w"], 0)], axis=1)
    for n, part in enumerate(np.split(in_w, [WAYS[0]], axis=1)):
        d[f"w_in{n}"] = np.tile(part.transpose(2, 1, 0), (P, 1, 1, 1))
    gamma = np.concatenate([rat_in["attn_g"], rat_in["mlp_g"]]).reshape(5, H)
    beta = np.concatenate([rat_in["attn_b"], rat_in["mlp_b"]]).reshape(5, H)
    gb = np.stack([_h_order(gamma, 1), _h_order(beta, 1)], axis=-1)
    d["gb"] = gb.reshape(5, HH, P, 2).transpose(2, 1, 0, 3)
    d["wqkv"] = _tiles(_h_order(rat_in["qkv"], 2).reshape(3 * H, H).T)
    d["ctx"] = _tiles(_h_order(ctx, 2).transpose(2, 0, 1))
    for n, w in enumerate(rat_out):
        ab, bias = w["wab"], w["wab_b"]
        def by_c(a):
            return a.reshape(RH, C - 1, *a.shape[1:]).swapaxes(0, 1).reshape(a.shape)
        rows = [_h_order(w["wod"][:H], 0), by_c(ab[:NA]), by_c(ab[NA:2 * NA]), ab[2 * NA:], w["wod"][H:]]
        d[f"wcat{n}"] = _tiles(np.concatenate(rows).T)
        row = np.concatenate([by_c(bias[:NA]), by_c(bias[NA:2 * NA]), bias[2 * NA:], np.zeros(DR, bias.dtype)])
        d[f"bias_ab{n}"] = np.tile(row, (P, 1))
        d[f"dut{n}"] = np.concatenate([_h_order(w["du"], 0).T, _h_order(w["du_b"], 0)[None]])
    for k, w in ffn.items():
        if k.endswith("w2"):
            d[k] = _f_order(w, 0).T.reshape(JT, P, HID)
        else:
            d[k] = _f_order(w, 1).reshape(JT, P, KF, P).transpose(0, 3, 2, 1).reshape(JT, P, HID)
    d["ident"] = np.eye(P, dtype=np.float32)
    q, k = np.arange(P)[:, None], np.arange(P)[None, :]
    d["cmask"] = np.where(k > q, np.float32(MASKED), np.float32(0)).astype(np.float32)
    half = np.arange(HALF, dtype=np.float32) / np.float32(HALF)
    d["inv_freq"] = np.tile((np.float32(1) / np.power(np.float32(10000), half)).astype(np.float32), (P, 1))
    return {k: np.ascontiguousarray(v) for k, v in d.items()}


def kernel(**inputs):
    import concourse.bacc as bacc
    from concourse.bass_utils import run_bass_kernel_spmd

    i = {k: np.asarray(v) for k, v in inputs.items()}
    a = {k[len("L0_xattn_"):]: v for k, v in i.items() if k.startswith("L0_xattn_")}
    d = _device_arrays(
        i["x"], i["pos_BxS"], i["ctx_1024"],
        {"attn_w": a["attn_read_w"], "attn_g": a["attn_read_g"], "attn_b": a["attn_read_b"], "qkv": a["qkv_w"],
         "mlp_w": a["mlp_read_w"], "mlp_g": a["mlp_read_g"], "mlp_b": a["mlp_read_b"]},
        [{"wod": a[f"{n}_wod_w"], "wab": a[f"{n}_wab_w"], "wab_b": a[f"{n}_wab_b"], "du": a[f"{n}_du_w"],
          "du_b": a[f"{n}_du_b"]} for n in ("attn", "mlp")],
        {k[len("L0_ffn_"):]: v for k, v in i.items() if k.startswith("L0_ffn_")})
    nc = bacc.Bacc("TRN2", target_bir_lowering=False, num_devices=1)
    arrays = {f"in_{k}": v for k, v in d.items()}
    aps = {k: nc.dram_tensor(f"in_{k}", v.shape, mybir.dt.from_np(v.dtype), kind="ExternalInput").ap() for k, v in d.items()}
    out = nc.dram_tensor("out", (TILES, P, HID), F32, kind="ExternalOutput").ap()
    bass_layer(nc, aps, out)
    r = run_bass_kernel_spmd(nc, [arrays], core_ids=[0])
    y = np.asarray(r.results[0]["out"]).reshape(BATCH, SEQ, C, RH, HS)
    return np.ascontiguousarray(y.transpose(0, 1, 4, 3, 2)).reshape(BATCH, SEQ, HID)
```
